# Optimizing a Trainium2 kernel written in Bass

```python
import numpy as np
import jax
import jax.numpy as jnp

def _softmax(x, axis=-1):
    return jax.nn.softmax(x, axis=axis)

def _gelu(x):
    return jax.nn.gelu(x, approximate=True)

def _silu(x):
    return jax.nn.silu(x)

def _sigmoid(x):
    return jax.nn.sigmoid(x)

def _layernorm(x, axis=-1, eps=1e-05):
    m = jnp.mean(x, axis=axis, keepdims=True)
    v = jnp.var(x, axis=axis, keepdims=True)
    return (x - m) / jnp.sqrt(v + eps)

def _scatter_add(tgt, idx, src, axis=0):
    return tgt.at[idx].add(src)

def _segment_sum(src, seg, n):
    return jax.ops.segment_sum(src, seg, n)
kernel_name = 'mk_gnn_preln_d2_gnn_r32_b5c841'

def setup_inputs(seed: int=0):
    np.random.seed(seed)
    _w = jnp.asarray

    def _rec_inputs():
        import jax
        import jax.numpy as jnp
        _gk = jax.random.key(seed)
        x = -3.195e-05 + 0.1 * jax.random.normal(jax.random.fold_in(_gk, 1), (3125, 32), jnp.float32)
        src = jax.random.randint(jax.random.fold_in(_gk, 2), (100000,), 0, 3125, jnp.int32)
        dst = jax.random.randint(jax.random.fold_in(_gk, 3), (100000,), 0, 3125, jnp.int32)
        _o = jnp.argsort(dst, stable=True)
        src = src[_o]
        dst = dst[_o]
        edge_attr_3 = jax.random.uniform(jax.random.fold_in(_gk, 11), (100000, 3), jnp.float32, 0.0, 0.999998)
        return (x, src, dst, edge_attr_3)
    x, src, dst, edge_attr_3 = _rec_inputs()

    def _L0_gnn_setup():
        import jax, jax.numpy as jnp
        import numpy as np
        N_LAYERS = 3
        N_NODES = 15625
        N_EDGES = 78125
        EMBED_DIM = 32
        key = jax.random.key(seed)
        k_w, k_e = jax.random.split(key)
        weight = jax.random.normal(k_w, (N_NODES, EMBED_DIM), dtype=jnp.float32) * 0.1
        edge_index = jax.random.randint(k_e, (2, N_EDGES), 0, N_NODES, dtype=jnp.int32)
        return {'weight': weight, 'edge_index': edge_index}
    _L0_gnn_all = _L0_gnn_setup()
    _L0_gnn_in = {k: v for k, v in _L0_gnn_all.items() if k in ()}
    del _L0_gnn_all

    def _L1_gnn_setup():
        import jax, jax.numpy as jnp
        import numpy as np
        D = 3
        KS = 5
        K = KS ** D
        S = 2 ** D
        _COMBOS = np.array([[s >> d & 1 for d in range(D)] for s in range(S)], dtype=np.int32)
        _STRIDES = np.array([KS ** (D - 1 - d) for d in range(D)], dtype=np.int32)

        def spline_basis(pseudo):
            pos = pseudo * (KS - 1)
            i0 = jnp.clip(jnp.floor(pos), 0, KS - 2).astype(jnp.int32)
            frac = pos - i0
            combos = jnp.asarray(_COMBOS)
            basis = jnp.prod(jnp.where(combos[None] == 1, frac[:, None, :], 1.0 - frac[:, None, :]), axis=-1)
            idx = jnp.sum((i0[:, None, :] + combos[None]) * jnp.asarray(_STRIDES)[None, None, :], axis=-1)
            return (basis, idx)

        def spline_conv(x, row, col, basis, idx, W, b):
            N = x.shape[0]
            Fout = W.shape[2]
            z = jnp.einsum('ni,kio->nko', x, W).reshape(N * K, Fout)
            gathered = z[col[:, None] * K + idx]
            msg = jnp.einsum('es,eso->eo', basis, gathered)
            out = jax.ops.segment_sum(msg, row, num_segments=N)
            deg = jax.ops.segment_sum(jnp.ones_like(msg[:, 0]), row, num_segments=N)
            return out / jnp.maximum(deg, 1.0)[:, None] + b
        key = jax.random.key(seed)
        ks = jax.random.split(key, 13)
        N, E, Fin, Fout = (625, 10000, 32, 32)

        def u(k, shape, size):
            bound = 1.0 / np.sqrt(size)
            return jax.random.uniform(k, shape, jnp.float32, -bound, bound)
        return dict(x=jax.random.normal(ks[0], (N, Fin), jnp.float32), edge_index=jax.random.randint(ks[1], (2, E), 0, N, dtype=jnp.int32), pseudo=jax.random.uniform(ks[2], (E, D), jnp.float32), stn1_w=u(ks[3], (K, 1, 64), 1 * S), stn1_b=u(ks[4], (64,), 1 * S), stn2_w=u(ks[5], (K, 64, 64), 64 * S), stn2_b=u(ks[6], (64,), 64 * S), stn3_w=u(ks[7], (64, 64), 64), stn3_b=u(ks[8], (64,), 64), stn4_w=u(ks[9], (64, 3), 64), stn4_b=u(ks[10], (3,), 64), conv_w=u(ks[11], (K, Fin, Fout), Fin * S), conv_b=u(ks[12], (Fout,), Fin * S))
    _L1_gnn_all = _L1_gnn_setup()
    _L1_gnn_in = {k: v for k, v in _L1_gnn_all.items() if k in ('stn1_w', 'stn1_b', 'stn2_w', 'stn2_b', 'stn3_w', 'stn3_b', 'stn4_w', 'stn4_b', 'conv_w', 'conv_b')}
    del _L1_gnn_all
    return {'x': x, 'src': src, 'dst': dst, 'edge_attr_3': edge_attr_3, 'L1_gnn_stn1_w': _L1_gnn_in['stn1_w'], 'L1_gnn_stn1_b': _L1_gnn_in['stn1_b'], 'L1_gnn_stn2_w': _L1_gnn_in['stn2_w'], 'L1_gnn_stn2_b': _L1_gnn_in['stn2_b'], 'L1_gnn_stn3_w': _L1_gnn_in['stn3_w'], 'L1_gnn_stn3_b': _L1_gnn_in['stn3_b'], 'L1_gnn_stn4_w': _L1_gnn_in['stn4_w'], 'L1_gnn_stn4_b': _L1_gnn_in['stn4_b'], 'L1_gnn_conv_w': _L1_gnn_in['conv_w'], 'L1_gnn_conv_b': _L1_gnn_in['conv_b']}

def reference(x, src, dst, edge_attr_3, L1_gnn_stn1_w, L1_gnn_stn1_b, L1_gnn_stn2_w, L1_gnn_stn2_b, L1_gnn_stn3_w, L1_gnn_stn3_b, L1_gnn_stn4_w, L1_gnn_stn4_b, L1_gnn_conv_w, L1_gnn_conv_b):
    import jax
    import jax.numpy as jnp

    def _L0_gnn_ref(weight, edge_index):
        import jax, jax.numpy as jnp
        import numpy as np
        N_LAYERS = 3
        N_NODES = 15625
        N_EDGES = 78125
        EMBED_DIM = 32
        src, dst = (edge_index[0], edge_index[1])
        n = weight.shape[0]
        deg = jax.ops.segment_sum(jnp.ones(src.shape, dtype=weight.dtype), dst, num_segments=n)
        deg_inv_sqrt = jnp.where(deg > 0, jax.lax.rsqrt(deg), jnp.zeros((), weight.dtype))
        norm = deg_inv_sqrt[src] * deg_inv_sqrt[dst]
        x = weight
        acc = weight
        for _ in range(N_LAYERS):
            msgs = norm[:, None] * x[src]
            x = jax.ops.segment_sum(msgs, dst, num_segments=n)
            acc = acc + x
        return acc / (N_LAYERS + 1)

    def _L1_gnn_ref(x, edge_index, pseudo, stn1_w, stn1_b, stn2_w, stn2_b, stn3_w, stn3_b, stn4_w, stn4_b, conv_w, conv_b):
        import jax, jax.numpy as jnp
        import numpy as np
        D = 3
        KS = 5
        K = KS ** D
        S = 2 ** D
        _COMBOS = np.array([[s >> d & 1 for d in range(D)] for s in range(S)], dtype=np.int32)
        _STRIDES = np.array([KS ** (D - 1 - d) for d in range(D)], dtype=np.int32)

        def spline_basis(pseudo):
            pos = pseudo * (KS - 1)
            i0 = jnp.clip(jnp.floor(pos), 0, KS - 2).astype(jnp.int32)
            frac = pos - i0
            combos = jnp.asarray(_COMBOS)
            basis = jnp.prod(jnp.where(combos[None] == 1, frac[:, None, :], 1.0 - frac[:, None, :]), axis=-1)
            idx = jnp.sum((i0[:, None, :] + combos[None]) * jnp.asarray(_STRIDES)[None, None, :], axis=-1)
            return (basis, idx)

        def spline_conv(x, row, col, basis, idx, W, b):
            N = x.shape[0]
            Fout = W.shape[2]
            z = jnp.einsum('ni,kio->nko', x, W).reshape(N * K, Fout)
            gathered = z[col[:, None] * K + idx]
            msg = jnp.einsum('es,eso->eo', basis, gathered)
            out = jax.ops.segment_sum(msg, row, num_segments=N)
            deg = jax.ops.segment_sum(jnp.ones_like(msg[:, 0]), row, num_segments=N)
            return out / jnp.maximum(deg, 1.0)[:, None] + b
        N = x.shape[0]
        row, col = (edge_index[0], edge_index[1])
        basis, idx = spline_basis(pseudo)
        h = jnp.ones((N, 1), x.dtype)
        h = jax.nn.elu(spline_conv(h, row, col, basis, idx, stn1_w, stn1_b))
        h = jax.nn.elu(spline_conv(h, row, col, basis, idx, stn2_w, stn2_b))
        h = jax.nn.elu(h @ stn3_w + stn3_b)
        t = h @ stn4_w + stn4_b
        new_pseudo = jnp.clip(pseudo + t[col] - t[row], 0.0, 1.0)
        basis2, idx2 = spline_basis(new_pseudo)
        return spline_conv(x, row, col, basis2, idx2, conv_w, conv_b)
    edge_index = jnp.stack([src, dst])
    h = jnp.maximum(_layernorm(x, axis=-1), 0.0)
    x = x + _L0_gnn_ref(h, edge_index)
    h = jnp.maximum(_layernorm(x, axis=-1), 0.0)
    x = x + _L1_gnn_ref(h, edge_index, edge_attr_3, L1_gnn_stn1_w, L1_gnn_stn1_b, L1_gnn_stn2_w, L1_gnn_stn2_b, L1_gnn_stn3_w, L1_gnn_stn3_b, L1_gnn_stn4_w, L1_gnn_stn4_b, L1_gnn_conv_w, L1_gnn_conv_b)
    return x

_drawn_inputs = setup_inputs


def setup_inputs(seed=0):
    import zlib

    import numpy as np

    out = dict(_drawn_inputs(seed))
    spreads = {}
    factors = {'L1_gnn_stn1_w': 8.0,
     'L1_gnn_stn1_b': 8.0,
     'L1_gnn_stn2_w': 8.0,
     'L1_gnn_stn2_b': 8.0,
     'L1_gnn_stn3_w': 8.0,
     'L1_gnn_stn3_b': 8.0,
     'L1_gnn_stn4_w': 8.0,
     'L1_gnn_stn4_b': 8.0}
    for name, (base, spread) in spreads.items():
        noise = np.random.default_rng([zlib.crc32(name.encode()), seed]).standard_normal(out[name].shape)
        drawn = base * np.exp(spread * noise) if base else spread * noise
        out[name] = jnp.asarray(drawn.astype(out[name].dtype))
    for name, factor in factors.items():
        out[name] = (out[name] * factor).astype(out[name].dtype)
    return out
```

```python
from contextlib import ExitStack

import concourse.bass as bass
from concourse import mybir

F32 = mybir.dt.float32
BF16 = mybir.dt.bfloat16
I32 = mybir.dt.int32
I16 = mybir.dt.int16
ALU = mybir.AluOpType
ACT = mybir.ActivationFunctionType
AX = mybir.AxisListType.X

P = 128
N = 3125
NT = -(-N // P)
NP = NT * P
NREST = N - (NT - 1) * P
E = 100000
EP = 125
EC = E // EP
HALF = 8
BODY = 2 * HALF
T = -(-(E // P + NT) // BODY) * BODY
TRIPS = T // BODY
D = 3
KS = 5
K = KS ** D
C = 32
H1 = 64
LAYERS = 3
REC = 8
CELLS = 4 * KS * 4
BANK = 512
EPS = 1e-5


class Chain:

    def __init__(self, eng, sem):
        self.eng, self.sem, self.base, self.off, self.k = eng, sem, 0, 0, 0

    def link(self, ins):
        ins.then_inc(self.sem, 1)
        self.k += 1
        self.eng.wait_ge(self.sem, self.off + self.k)

    def enter(self, i, steps):
        self.base = self.off + self.k
        self.steps, self.off, self.k = steps, self.base + i * steps, 0

    def leave(self, trips):
        assert self.k == self.steps, (self.k, self.steps)
        self.off, self.k = self.base + trips * self.steps, 0


def bcast(ap, dim, n):
    v = ap.unsqueeze(dim)
    shape = list(v.shape)
    shape[dim] = n
    return v.broadcast_to(shape)


def gnn(nc, x, src, dst, edge_attr_3, w1, b1, w2, b2, w3, b3, w4, b4, wc, bc, out):
    recs = nc.dram_tensor("recs", (P * T, REC), F32, kind="Internal").ap()
    corners2 = nc.dram_tensor("corners2", (NP * CELLS, 4 * H1), F32, kind="Internal").ap()
    corners3 = nc.dram_tensor("corners3", (NP * CELLS, 4 * C), F32, kind="Internal").ap()
    ytab = nc.dram_tensor("ytab", (NP, 3 * C), BF16, kind="Internal").ap()

    with ExitStack() as whole:
        scopes = [whole]

        def sb(name, shape, dt=F32):
            return scopes[-1].enter_context(nc.sbuf_tensor(name, shape, dt))

        def ps(name, shape, dt=F32):
            return scopes[-1].enter_context(nc.psum_tensor(name, shape, dt))

        def sem(name):
            return scopes[-1].enter_context(nc.semaphore(name))

        class Phase:

            def __enter__(self):
                scopes.append(ExitStack())
                scopes[-1].__enter__()

            def __exit__(self, *a):
                scopes.pop().__exit__(*a)

        iota128 = sb("iota128", [P, P])
        pidx = sb("pidx", [P, 1])
        ident = sb("ident", [P, P])
        ones = sb("ones", [P, P])
        bucket = sb("bucket", [P, T], I32)
        esrc = sb("esrc", [P, T])
        srclo = sb("srclo", [P, T])
        edst = sb("edst", [P, T])
        dstlo = sb("dstlo", [P, T])
        dsthi = sb("dsthi", [P, T])
        pseudo = sb("pseudo", [P, T, D])
        acc = sb("acc", [P, 2, NT * (K + 1)])
        rdeg = sb("rdeg", [P, NT])
        dis = sb("dis", [P, NT])
        xn = sb("xn", [P, NT, C])
        h = sb("h", [P, NT, H1])

        with Phase():
            esi = sb("esi", [EP, EC], I32)
            edi = sb("edi", [EP, EC], I32)
            eps_in = sb("eps_in", [EP, EC, D])
            hi_i = sb("hi_i", [EP, EC], I32)
            key = sb("key", [EP, EC])
            eq = sb("eq", [EP, EC])
            cum = sb("cum", [EP, EC])
            zero = sb("zero", [EP, EC])
            mine = sb("mine", [EP, EC])
            pos = sb("pos", [EP, EC])
            posi = sb("posi", [EP, EC], I32)
            posh = sb("posh", [EP, EC], I32)
            posf = sb("posf", [EP, EC])
            rec = sb("rec", [EP, EC, REC])
            pad = sb("pad", [P, T, REC])
            tot = sb("tot", [EP, NT])
            tri = sb("tri", [P, P])
            cnti = sb("cnti", [P, NT], I32)
            tiles = sb("tiles", [P, NT])
            tend = sb("tend", [P, NT])
            tstart = sb("tstart", [P, NT])
            off = sb("off", [EP, NT])
            iotat = sb("iotat", [P, T])
            bf = sb("bf", [P, T])
            stage_i = sb("stage_i", [EP, BODY], I32)
            stage_r = sb("stage_r", [EP, BODY, REC])
            count_ps = ps("count_ps", [P, 2, BANK])
            loaded, iotas, step, tot_ready, counts = (sem(n) for n in ("loaded", "iotas", "step", "tot_ready", "counts"))
            padded, pad_ready, staged, gate = (sem(n) for n in ("padded", "pad_ready", "staged", "gate"))
            stored = [sem(f"stored{i}") for i in range(2)]
            with nc.Block() as block:

                @block.sync
                def _(sp):
                    sp.dma_start(esi[:, :], src.rearrange("(p c) -> p c", p=EP)).then_inc(loaded, 16)
                    sp.dma_start(edi[:, :], dst.rearrange("(p c) -> p c", p=EP)).then_inc(loaded, 16)
                    sp.dma_start(eps_in[:, :, :], edge_attr_3.rearrange("(p c) d -> p c d", p=EP)).then_inc(loaded, 16)
                    sp.wait_ge(pad_ready, 1)
                    sp.dma_start(recs.rearrange("(p t) r -> p (t r)", p=P), pad[:, :, :].rearrange("p t r -> p (t r)")).then_inc(padded, 16)

                @block.tensor
                def _(pe):
                    pe.wait_ge(tot_ready, 1)
                    nc.tensor.matmul(count_ps[0:EP, 0, 0:NT], tri[0:EP, 0:EP], tot[:, :], start=True, stop=True)
                    nc.tensor.matmul(count_ps[:, 1, 0:NT], ones[0:EP, :], tot[:, :], start=True, stop=True).then_inc(counts, 1)

                @block.vector
                def _(v):
                    ch = Chain(v, step)
                    ch.link(v.memset(pad[:, :, :], 0.0))
                    v.memset(pad[:, :, 0:2], -1.0).then_inc(pad_ready, 1)
                    v.memset(ones[:, :], 1.0)
                    v.memset(zero[:, :], 0.0)
                    v.memset(rec[:, :, :], 0.0)
                    v.memset(bf[:, :], -1.0)
                    v.memset(acc[:, :, :], 0.0)
                    ch.link(v.memset(pos[:, :], 0.0))
                    v.wait_ge(iotas, 3)
                    v.tensor_scalar(ident[:, :], iota128[:, :], pidx[:, 0:1], None, ALU.is_equal)
                    ch.link(v.tensor_scalar(tri[:, :], iota128[:, :], pidx[:, 0:1], None, ALU.is_gt))
                    v.wait_ge(loaded, 48)
                    v.tensor_copy(rec[:, :, 0], esi[:, :])
                    v.tensor_copy(rec[:, :, 1], edi[:, :])
                    v.tensor_copy(rec[:, :, 2:2 + D], eps_in[:, :, :])
                    ch.link(v.tensor_scalar(hi_i[:, :], esi[:, :], 7, None, ALU.arith_shift_right))
                    ch.link(v.tensor_copy(key[:, :], hi_i[:, :]))
                    for b in range(NT):
                        ins = v.tensor_scalar(eq[:, :], key[:, :], float(b), None, ALU.is_equal, ALU.add, accum_out=tot[:, b:b + 1])
                        ch.link(ins)
                    v.sem_inc(tot_ready, 1)
                    v.wait_ge(counts, 1)
                    ch.link(v.tensor_scalar(cnti[:, :], count_ps[:, 1, 0:NT], float(P - 1), None, ALU.add))
                    ch.link(v.tensor_scalar(cnti[:, :], cnti[:, :], 7, None, ALU.arith_shift_right))
                    ch.link(v.tensor_copy(tiles[:, :], cnti[:, :]))
                    ch.link(v.tensor_tensor_scan(tend[:, :], ones[:, 0:NT], tiles[:, :], 0.0, ALU.mult, ALU.add))
                    ch.link(v.tensor_tensor(tstart[:, :], tend[:, :], tiles[:, :], ALU.subtract))
                    ch.link(v.tensor_scalar(off[:, :], tstart[0:EP, :], float(P), -1.0, ALU.mult, ALU.add))
                    ch.link(v.tensor_tensor(off[:, :], count_ps[0:EP, 0, 0:NT], off[:, :], ALU.add))
                    for b in range(NT):
                        ch.link(v.tensor_scalar(eq[:, :], key[:, :], float(b), None, ALU.is_equal))
                        ch.link(v.tensor_tensor_scan(cum[:, :], eq[:, :], zero[:, :], 0.0, ALU.add, ALU.add))
                        ch.link(v.scalar_tensor_tensor(mine[:, :], cum[:, :], off[:, b:b + 1], eq[:, :], ALU.add, ALU.mult))
                        ch.link(v.tensor_tensor(pos[:, :], pos[:, :], mine[:, :], ALU.add))
                    ch.link(v.tensor_copy(posi[:, :], pos[:, :]))
                    ch.link(v.tensor_scalar(posh[:, :], posi[:, :], 7, None, ALU.arith_shift_right))
                    ch.link(v.tensor_scalar(posi[:, :], posi[:, :], P - 1, None, ALU.bitwise_and))
                    v.tensor_copy(posf[:, :], posi[:, :])
                    ch.link(v.tensor_copy(mine[:, :], posh[:, :]))
                    ch.link(v.scalar_tensor_tensor(pos[:, :], posf[:, :], float(T), mine[:, :], ALU.mult, ALU.add))
                    ch.link(v.tensor_copy(posi[:, :], pos[:, :]))
                    for b in range(NT):
                        ch.link(v.scalar_tensor_tensor(bf[:, :], iotat[:, :], tstart[:, b:b + 1], bf[:, :], ALU.is_ge, ALU.add))
                    ch.link(v.tensor_copy(bucket[:, :], bf[:, :]))
                    def stage(turn, g):
                        v.tensor_copy(stage_i[:, g * HALF:(g + 1) * HALF], posi[:, bass.ds(turn * BODY + g * HALF, HALF)])
                        v.tensor_copy(stage_r[:, g * HALF:(g + 1) * HALF, :], rec[:, bass.ds(turn * BODY + g * HALF, HALF), :]).then_inc(staged, 1)

                    stage(0, 0)
                    stage(0, 1)
                    with v.Fori(0, EC // BODY - 1) as i:
                        for g in range(2):
                            v.wait_ge(stored[g], (i + 1) * (16 * HALF))
                            stage(i + 1, g)

                @block.gpsimd
                def _(pool):
                    pool.iota(iota128[:, :], [[1, P]], base=0, channel_multiplier=0, allow_small_or_imprecise_dtypes=True).then_inc(iotas, 1)
                    pool.iota(pidx[:, :], [[0, 1]], base=0, channel_multiplier=1, allow_small_or_imprecise_dtypes=True).then_inc(iotas, 1)
                    pool.iota(iotat[:, :], [[1, T]], base=0, channel_multiplier=0, allow_small_or_imprecise_dtypes=True).then_inc(iotas, 1)
                    pool.wait_ge(padded, 16)
                    with pool.Fori(0, EC // BODY) as i:
                        for g in range(2):
                            pool.wait_ge(staged, 2 * i + g + 1)
                            pool.sem_inc(gate, 1)
                            for j in range(g * HALF, (g + 1) * HALF):
                                pool.indirect_dma_start(recs, bass.IndirectOffsetOnAxis(ap=stage_i[:, j:j + 1], axis=0),
                                                        stage_r[:, j, :], None).then_inc(stored[g], 16)
                    for g in range(2):
                        pool.wait_ge(stored[g], EC // BODY * HALF * 16)

        def corner_tables(v, ch, i0, fr, fr0, weight, cidx, tmp):
            ch.link(v.tensor_scalar(fr[:, :, :], pseudo[:, :, :], float(KS - 1), None, ALU.mult))
            ch.link(v.tensor_scalar(i0[:, :, :], fr[:, :, :], 1.0, None, ALU.is_ge))
            for knot in range(2, KS - 1):
                ch.link(v.scalar_tensor_tensor(i0[:, :, :], fr[:, :, :], float(knot), i0[:, :, :], ALU.is_ge, ALU.add))
            ch.link(v.tensor_tensor(fr[:, :, :], fr[:, :, :], i0[:, :, :], ALU.subtract))
            ch.link(v.tensor_scalar(fr0[:, :, :], fr[:, :, :], -1.0, 1.0, ALU.mult, ALU.add))
            w = weight[:, :, :].rearrange("p t (y x z) -> p t y x z", y=2, x=2)
            side = (fr0, fr)
            for cy in range(2):
                for cx in range(2):
                    v.tensor_tensor(w[:, :, cy, cx, 1], side[cx][:, :, 0], side[cy][:, :, 1], ALU.mult)
            for cy in range(2):
                for cx in range(2):
                    last = v.tensor_tensor(w[:, :, cy, cx, 0], side[cx][:, :, 0], side[cy][:, :, 1], ALU.mult)
            ch.link(last)
            for cz in range(2):
                for c in range(4):
                    cc = w[:, :, c // 2, c % 2, cz]
                    last = v.tensor_tensor(cc, cc, side[cz][:, :, 2], ALU.mult)
            ch.link(last)
            ch.link(v.tensor_scalar(tmp[:, :], edst[:, :], 0.0, float(CELLS), ALU.max, ALU.mult))
            for d, stride in ((0, KS * 4), (1, 4), (2, 1)):
                ch.link(v.scalar_tensor_tensor(tmp[:, :], i0[:, :, d], float(stride), tmp[:, :], ALU.mult, ALU.add))
            v.tensor_copy(cidx[:, :, 0], tmp[:, :])
            ch.link(v.tensor_scalar(cidx[:, :, 1], tmp[:, :], 4.0, None, ALU.add))

        def refine(v, ch, s, a, tmp):
            ch.link(v.tensor_tensor(tmp, s, s, ALU.mult))
            ch.link(v.tensor_tensor(tmp, tmp, a, ALU.mult))
            ch.link(v.tensor_scalar(tmp, tmp, -0.5, 1.5, ALU.mult, ALU.add))
            ch.link(v.tensor_tensor(s, s, tmp, ALU.mult))

        def fold(v, acc, width, result, bucket_of, added, n, j):
            v.wait_ge(added, n + (j + 1))
            a = acc[:, j % 2, bass.ds(bucket_of * width, width)]
            v.tensor_tensor(a, result, a, ALU.add).then_inc(added, 1)

        with Phase():
            hat = sb("hat", [P, T, D, KS])
            yz = sb("yz", [P, 2, HALF, KS, KS])
            basis = sb("basis", [P, 2, HALF, K + 1])
            own = sb("own", [P, 2, HALF, P])
            dlo = sb("dlo", [P, 2, HALF, P], BF16)
            dhi = sb("dhi", [P, 2, HALF, NT], BF16)
            deg = sb("deg", [P, NT])
            rec_deg = sb("rec_deg", [P, NT])
            nt_tmp = sb("nt_tmp", [P, NT])
            has = sb("has", [P, NT])
            zb = sb("zb", [P, P], BF16)
            with Phase():
                back = sb("back", [P, T, REC])
                ti = sb("ti", [P, T], I32)
                t2 = sb("t2", [P, T], I32)
                loaded, step = sem("loaded2"), sem("step2")
                with nc.Block() as block:

                    @block.sync
                    def _(sp):
                        sp.dma_start(back[:, :, :].rearrange("p t r -> p (t r)"), recs.rearrange("(p t) r -> p (t r)", p=P)).then_inc(loaded, 16)

                    @block.vector
                    def _(v):
                        ch = Chain(v, step)
                        v.wait_ge(loaded, 16)
                        v.tensor_copy(esrc[:, :], back[:, :, 0])
                        v.tensor_copy(edst[:, :], back[:, :, 1])
                        v.tensor_copy(pseudo[:, :, :], back[:, :, 2:2 + D])
                        v.memset(basis[:, :, :, K:K + 1], 1.0)
                        v.memset(zb[:, :], 0.0)
                        ch.link(v.tensor_copy(ti[:, :], back[:, :, 0]))
                        ch.link(v.tensor_scalar(ti[:, :], ti[:, :], P - 1, None, ALU.bitwise_and))
                        ch.link(v.tensor_copy(srclo[:, :], ti[:, :]))
                        v.tensor_scalar(edst[:, :], edst[:, :], 0.0, None, ALU.add)
                        ch.link(v.tensor_scalar(dsthi[:, :], esrc[:, :], 0.0, 1024.0, ALU.min, ALU.mult))
                        ch.link(v.tensor_tensor(srclo[:, :], srclo[:, :], dsthi[:, :], ALU.add))
                        ch.link(v.tensor_copy(ti[:, :], back[:, :, 1]))
                        v.tensor_scalar(t2[:, :], ti[:, :], 7, None, ALU.arith_shift_right)
                        ch.link(v.tensor_scalar(ti[:, :], ti[:, :], P - 1, None, ALU.bitwise_and))
                        v.tensor_copy(dstlo[:, :], ti[:, :])
                        ch.link(v.tensor_copy(dsthi[:, :], t2[:, :]))
                        for k in range(KS):
                            ch.link(v.tensor_scalar(hat[:, :, :, k], pseudo[:, :, :], float(KS - 1), -float(k), ALU.mult, ALU.add))
                        hf = hat[:, :, :, :].rearrange("p t d k -> p (t d k)")
                        ch.link(v.scalar_tensor_tensor(hf, hf, -1.0, hf, ALU.mult, ALU.min))
                        ch.link(v.tensor_scalar(hf, hf, 1.0, 0.0, ALU.add, ALU.max))

            sums_ps = ps("sums_ps", [P, 2, 2, BANK])
            deg_ps = ps("deg_ps", [P, BANK])
            made, used, added, step, degs = (sem(n) for n in ("made", "used", "added", "step3", "degs"))
            with nc.Block() as block:

                @block.vector
                def _(v):
                    ch = Chain(v, step)
                    v.sem_inc(added, 2)

                    def make(n, g):
                        v.wait_ge(used, n + 1)
                        s = bass.ds(n * HALF, HALF)
                        hx, hy, hz = (hat[:, s, d, :] for d in range(D))
                        ch.link(v.tensor_tensor(yz[:, g, :, :, :], bcast(hy, 3, KS), bcast(hz, 2, KS), ALU.mult))
                        yzf = yz[:, g, :, :, :].rearrange("p t y z -> p t (y z)")
                        v.tensor_tensor(basis[:, g, :, 0:K].rearrange("p t (x r) -> p t x r", x=KS),
                                        bcast(hx, 3, KS * KS), bcast(yzf, 2, KS), ALU.mult)
                        v.tensor_tensor(dhi[:, g, :, :], bcast(iota128[:, 0:NT], 1, HALF), bcast(dsthi[:, s], 2, NT), ALU.is_equal)
                        for j in range(HALF):
                            e = bass.ds(n * HALF + j, 1)
                            v.tensor_scalar(own[:, g, j, :], iota128[:, :], srclo[:, e], None, ALU.is_equal)
                            last = v.tensor_scalar(dlo[:, g, j, :], iota128[:, :], dstlo[:, e], None, ALU.is_equal)
                        last.then_inc(made, 1)

                    def take(n, g):
                        v.wait_ge(used, n + 3)
                        for j in range(HALF):
                            b = v.value_load(bucket[0:1, bass.ds(n * HALF + j, 1)], min_val=0, max_val=NT - 1)
                            fold(v, acc, K + 1, sums_ps[:, g, j // 4, (j % 4) * (K + 1):(j % 4 + 1) * (K + 1)], b, added, n * HALF, j)

                    make(0, 0)
                    base = ch.off + ch.k
                    ch.off, ch.k = base, 0
                    with v.Fori(0, TRIPS - 1) as i:
                        ch.off, ch.k = base + i * 2, 0
                        make(2 * i + 1, 1)
                        take(2 * i, 0)
                        make(2 * i + 2, 0)
                        take(2 * i + 1, 1)
                    ch.off, ch.k = base + (TRIPS - 1) * 2, 0
                    make(2 * TRIPS - 1, 1)
                    take(2 * TRIPS - 2, 0)
                    take(2 * TRIPS - 1, 1)
                    v.wait_ge(added, 2 + T)
                    ch.link(v.tensor_tensor(acc[:, 0, :], acc[:, 0, :], acc[:, 1, :], ALU.add))
                    v.tensor_scalar(rdeg[:, :], acc[:, 0, :].rearrange("p (t k) -> p t k", k=K + 1)[:, :, K], 1.0, None, ALU.max)
                    v.wait_ge(degs, 1)
                    ch.link(v.tensor_scalar(deg[:, :], deg_ps[:, 0:NT], 1.0, None, ALU.max))
                    v.tensor_scalar(has[:, :], deg_ps[:, 0:NT], 0.0, None, ALU.is_gt)
                    ch.link(v.reciprocal(rdeg[:, :], rdeg[:, :]))
                    ch.link(v.reciprocal(rec_deg[:, :], deg[:, :]))
                    v.sem_inc(degs, 1)
                    v.wait_ge(degs, 3)
                    refine(v, ch, dis[:, :], deg[:, :], nt_tmp[:, :])
                    v.tensor_tensor(dis[:, :], dis[:, :], has[:, :], ALU.mult)

                @block.scalar
                def _(act):
                    act.wait_ge(degs, 2)
                    act.activation(dis[:, :], rec_deg[:, :], ACT.Sqrt).then_inc(degs, 1)

                @block.tensor
                def _(pe):
                    pe.matmul(deg_ps[:, 0:NT], zb[:, :], zb[:, 0:NT], start=True, stop=False)
                    pe.sem_inc(used, 2)

                    def sums(n, g):
                        pe.wait_ge(made, n + 1)
                        for j in range(HALF):
                            pe.matmul(deg_ps[:, 0:NT], dlo[:, g, j, :], dhi[:, g, j, :], start=False, stop=False)
                        for j in range(HALF):
                            last = pe.matmul(sums_ps[:, g, j // 4, (j % 4) * (K + 1):(j % 4 + 1) * (K + 1)],
                                             own[:, g, j, :], basis[:, g, j, :], start=True, stop=True)
                        last.then_inc(used, 1)

                    with pe.Fori(0, TRIPS) as i:
                        sums(2 * i, 0)
                        sums(2 * i + 1, 1)
                    pe.matmul(deg_ps[:, 0:NT], zb[:, :], zb[:, 0:NT], start=False, stop=True).then_inc(degs, 1)


        def linear(name, tile_of, kin, w, kout, result, scale=None):
            G = 5
            with Phase():
                turned = sb(name + "_turned", [kin, G * P])
                turned_ps = ps(name + "_turned_ps", [P, 2 * BANK])
                out_ps = ps(name + "_out_ps", [P, BANK])
                in_psum, in_sbuf, multiplied, kept = (sem(name + x) for x in ("_t", "_s", "_m", "_k"))
                with nc.Block() as block:

                    @block.tensor
                    def _(pe):
                        for i in range(NT // G):
                            for j in range(G):
                                last = pe.transpose(turned_ps[0:kin, j * P:(j + 1) * P], tile_of(i * G + j), ident[:, :])
                            last.then_inc(in_psum, 1)
                            pe.wait_ge(in_sbuf, i + 1)
                            pe.wait_ge(kept, i + 1)
                            for j in range(G):
                                last = pe.matmul(out_ps[:, j * kout:(j + 1) * kout], turned[:, j * P:(j + 1) * P], w, start=True, stop=True)
                            last.then_inc(multiplied, 1)

                    @block.scalar
                    def _(act):
                        with act.Fori(0, NT // G) as i:
                            act.wait_ge(in_psum, i + 1)
                            act.activation(turned[:, :], turned_ps[0:kin, 0:G * P], ACT.Copy).then_inc(in_sbuf, 1)

                    @block.vector
                    def _(v):
                        v.sem_inc(kept, 1)
                        with v.Fori(0, NT // G) as i:
                            v.wait_ge(multiplied, i + 1)
                            r = result[:, bass.ds(i * G, G), :]
                            o = out_ps[:, 0:G * kout].rearrange("p (t c) -> p t c", t=G)
                            if scale is None:
                                v.tensor_copy(r, o).then_inc(kept, 1)
                            else:
                                v.tensor_tensor(r, o, bcast(scale[:, bass.ds(i * G, G)], 2, kout), ALU.mult).then_inc(kept, 1)

        def bias_elu(name, u, bias):
            with Phase():
                low = sb(name + "_low", [P, NT, H1])
                step, cut, raised = sem(name + "_step"), sem(name + "_cut"), sem(name + "_raised")
                with nc.Block() as block:

                    @block.vector
                    def _(v):
                        ch = Chain(v, step)
                        ch.link(v.tensor_tensor(u, u, bcast(bias, 1, NT), ALU.add))
                        v.tensor_scalar(low[:, :, :], u, 0.0, None, ALU.min).then_inc(cut, 1)
                        v.wait_ge(raised, 1)
                        ch.link(v.tensor_scalar(u, u, 0.0, -1.0, ALU.max, ALU.add))
                        v.tensor_tensor(u, u, low[:, :, :], ALU.add)

                    @block.scalar
                    def _(act):
                        act.wait_ge(cut, 1)
                        act.activation(low[:, :, :], low[:, :, :], ACT.Exp).then_inc(raised, 1)

        def build_corners(name, f, nodes, w_dram, table):
            G = 5
            plane = KS * KS * f
            banks = -(-plane // BANK)
            with Phase():
                w = sb(name + "_w", [f, K * f])
                turned = sb(name + "_turned", [f, NT * P])
                with Phase():
                    turned_ps = ps(name + "_turned_ps", [P, 2, 2 * BANK])
                    in_psum, in_sbuf, loaded = (sem(name + x) for x in ("_t", "_s", "_l"))
                    with nc.Block() as block:

                        @block.sync
                        def _(sp):
                            sp.dma_start(w[:, :].rearrange("i (k o) -> i k o", k=K), w_dram.rearrange("k i o -> i k o")).then_inc(loaded, 16)
                            sp.wait_ge(loaded, 16)

                        @block.tensor
                        def _(pe):
                            for i in range(NT // G):
                                if i >= 2:
                                    pe.wait_ge(in_sbuf, i - 1)
                                for j in range(G):
                                    last = pe.transpose(turned_ps[0:f, i % 2, j * P:(j + 1) * P], nodes[:, i * G + j, 0:f], ident[:, :])
                                last.then_inc(in_psum, 1)

                        @block.scalar
                        def _(act):
                            for i in range(NT // G):
                                act.wait_ge(in_psum, i + 1)
                                act.activation(turned[:, i * G * P:(i + 1) * G * P], turned_ps[0:f, i % 2, 0:G * P], ACT.Copy).then_inc(in_sbuf, 1)

                mine = sb(name + "_mine", [f, P])
                placed, gate_p = sem(name + "_placed"), sem(name + "_gate_p")
                cube = sb(name + "_cube", [P, 4, KS, 4, 2, 2 * f])
                plane_ps = ps(name + "_plane_ps", [P, 2, banks * BANK])
                planes, by_act, by_dve = (sem(name + x) for x in ("_planes", "_by_act", "_by_dve"))
                stored = [sem(f"{name}_stored{i}") for i in range(4)]
                rows = table.rearrange("(t p x r) c -> t p x (r c)", t=NT, p=P, x=4)

                def spread(copy, kx, x, cx):
                    knots = plane_ps[:, kx % 2, 0:plane].rearrange("p (y z o) -> p y z o", y=KS, z=KS)
                    for cz in range(2):
                        last = copy(cube[:, x, :, :, cx, cz * f:(cz + 1) * f], knots[:, :, cz:cz + 4, :])
                    return last

                with nc.Block() as block:

                    @block.gpsimd
                    def _(pool):
                        pool.tensor_copy(mine[:, :], turned[:, 0:P]).then_inc(placed, 1)
                        with pool.Fori(1, NT) as i:
                            pool.wait_ge(planes, i * KS)
                            pool.sem_inc(gate_p, 1)
                            pool.tensor_copy(mine[:, :], turned[:, bass.ds(i * P, P)]).then_inc(placed, 1)

                    @block.tensor
                    def _(pe):
                        with pe.Fori(0, NT) as i:
                            pe.wait_ge(placed, i + 1)
                            for kx in range(KS):
                                if kx == 0:
                                    pe.wait_ge(by_dve, 4 * i + 1)
                                else:
                                    pe.wait_ge(by_act, 4 * i + kx)
                                for c in range(banks):
                                    n = min(BANK, plane - c * BANK)
                                    last = pe.matmul(plane_ps[:, kx % 2, c * BANK:c * BANK + n], mine[:, :],
                                                     w[:, kx * plane + c * BANK:kx * plane + c * BANK + n], start=True, stop=True)
                                last.then_inc(planes, 1)

                    def near(act, i, first):
                        for kx in range(4):
                            if not first:
                                act.wait_ge(stored[kx], i * 16)
                                act.wait_ge(by_dve, 4 * i + kx - 2)
                            act.wait_ge(planes, KS * i + kx + 1)
                            if not first:
                                act.sem_inc(gate_a, 1)
                            spread(lambda o, s: act.activation(o, s, ACT.Copy), kx, kx, 0).then_inc(by_act, 1)

                    def far(v, i, first):
                        for kx in range(1, KS):
                            if not first:
                                v.wait_ge(stored[kx - 1], i * 16)
                            if kx < 4:
                                v.wait_ge(by_act, 4 * i + kx + 2)
                                v.tensor_copy(cube[:, kx - 1, :, :, 1, :], cube[:, kx, :, :, 0, :]).then_inc(by_dve, 1)
                            else:
                                v.wait_ge(planes, KS * i + kx + 1)
                                spread(v.tensor_copy, kx, kx - 1, 1).then_inc(by_dve, 1)

                    gate_a = sem(name + "_gate_a")

                    @block.scalar
                    def _(act):
                        act.sem_inc(by_act, 1)
                        near(act, 0, True)
                        with act.Fori(1, NT) as i:
                            near(act, i, False)

                    @block.vector
                    def _(v):
                        v.sem_inc(by_dve, 1)
                        far(v, 0, True)
                        with v.Fori(1, NT) as i:
                            far(v, i, False)

                    @block.sync
                    def _(sp):
                        with sp.Fori(0, NT) as i:
                            for x in range(4):
                                sp.wait_ge(by_act, 4 * i + x + 2)
                                sp.wait_ge(by_dve, 4 * i + x + 2)
                                sp.dma_start(rows[i, :, x, :], cube[:, x, :, :, :, :].rearrange("p y z a b -> p (y z a b)")).then_inc(stored[x], 16)
                        for x in range(4):
                            sp.wait_ge(stored[x], 16 * NT)

        def spline(name, f, table):
            with Phase():
                weight = sb(name + "_weight", [P, T, 8])
                cidx = sb(name + "_cidx", [P, T, 2], I32)
                with Phase():
                    i0 = sb(name + "_i0", [P, T, D])
                    fr = sb(name + "_fr", [P, T, D])
                    fr0 = sb(name + "_fr0", [P, T, D])
                    tmp = sb(name + "_tmp", [P, T])
                    step = sem(name + "_step")
                    with nc.Block() as block:

                        @block.vector
                        def _(v):
                            v.memset(acc[:, :, :], 0.0)
                            corner_tables(v, Chain(v, step), i0, fr, fr0, weight, cidx, tmp)

                stage = sb(name + "_stage", [P, 2, HALF * 2], I32)
                rows = sb(name + "_rows", [P, 2, HALF, 2, 4 * f])
                msg = sb(name + "_msg", [P, 2, HALF, f])
                own = sb(name + "_own", [P, 2, HALF, P])
                sums_ps = ps(name + "_sums_ps", [P, 2, BANK])
                staged, made, used, added, step, gate = (sem(name + x) for x in ("_staged", "_made", "_used", "_added", "_step2", "_gate"))
                fetched = [sem(f"{name}_fetched{g}") for g in range(2)]
                with nc.Block() as block:

                    @block.gpsimd
                    def _(pool):
                        with pool.Fori(0, TRIPS) as i:
                            for g in range(2):
                                pool.wait_ge(staged, 2 * i + g + 1)
                                pool.sem_inc(gate, 1)
                                for j in range(HALF):
                                    for c in range(2):
                                        pool.indirect_dma_start(rows[:, g, j, c, :], None, table,
                                                                bass.IndirectOffsetOnAxis(ap=stage[:, g, 2 * j + c:2 * j + c + 1], axis=0)).then_inc(fetched[g], 16)

                    @block.tensor
                    def _(pe):
                        pe.sem_inc(used, 2)

                        def sums(n, g):
                            pe.wait_ge(made, n + 1)
                            for j in range(HALF):
                                last = pe.matmul(sums_ps[:, g, j * f:(j + 1) * f], own[:, g, j, :], msg[:, g, j, :], start=True, stop=True)
                            last.then_inc(used, 1)

                        with pe.Fori(0, TRIPS) as i:
                            sums(2 * i, 0)
                            sums(2 * i + 1, 1)

                    @block.vector
                    def _(v):
                        v.sem_inc(added, 2)

                        def put(n, g):
                            v.tensor_copy(stage[:, g, :], cidx[:, bass.ds(n * HALF, HALF), :].rearrange("p t c -> p (t c)")).then_inc(staged, 1)

                        def make(n, trip, g, more):
                            v.wait_ge(used, n + 1)
                            for j in range(HALF):
                                v.tensor_scalar(own[:, g, j, :], iota128[:, :], srclo[:, bass.ds(n * HALF + j, 1)], None, ALU.is_equal)
                            v.wait_ge(fetched[g], (trip + 1) * (2 * HALF * 16))
                            for s in range(8):
                                for j in range(HALF):
                                    row = rows[:, g, j, s // 4, (s % 4) * f:(s % 4 + 1) * f]
                                    wt = weight[:, bass.ds(n * HALF + j, 1), s]
                                    if s == 0:
                                        ins = v.tensor_scalar(msg[:, g, j, :], row, wt, None, ALU.mult)
                                    else:
                                        v.wait_ge(step, n * (8 * HALF) + (s - 1) * HALF + j + 1)
                                        ins = v.scalar_tensor_tensor(msg[:, g, j, :], row, wt, msg[:, g, j, :], ALU.mult, ALU.add)
                                    ins.then_inc(step, 1)
                            v.wait_ge(step, (n + 1) * (8 * HALF))
                            v.sem_inc(made, 1)
                            if more:
                                put(n + 2, g)

                        def take(n, g):
                            v.wait_ge(used, n + 3)
                            for j in range(HALF):
                                b = v.value_load(bucket[0:1, bass.ds(n * HALF + j, 1)], min_val=0, max_val=NT - 1)
                                fold(v, acc, f, sums_ps[:, g, j * f:(j + 1) * f], b, added, n * HALF, j)

                        put(0, 0)
                        put(1, 1)
                        make(0, 0, 0, True)
                        with v.Fori(0, TRIPS - 2) as i:
                            make(2 * i + 1, i, 1, True)
                            take(2 * i, 0)
                            make(2 * i + 2, i + 1, 0, True)
                            take(2 * i + 1, 1)
                        make(2 * TRIPS - 3, TRIPS - 2, 1, True)
                        take(2 * TRIPS - 4, 0)
                        make(2 * TRIPS - 2, TRIPS - 1, 0, False)
                        take(2 * TRIPS - 3, 1)
                        make(2 * TRIPS - 1, TRIPS - 1, 1, False)
                        take(2 * TRIPS - 2, 0)
                        take(2 * TRIPS - 1, 1)
                        v.wait_ge(added, 2 + T)
                        v.tensor_tensor(acc[:, 0, 0:NT * f], acc[:, 0, 0:NT * f], acc[:, 1, 0:NT * f], ALU.add)

        with Phase():
            w1s = sb("w1s", [K, H1])
            w3s = sb("w3s", [H1, H1])
            w4s = sb("w4s", [H1, D])
            bias = sb("bias", [P, 4, H1])
            tn = sb("tn", [P, 2, NT, D])
            loaded = sem("loaded3")
            with nc.Block() as block:

                @block.sync
                def _(sp):
                    sp.dma_start(w1s[:, :], w1.rearrange("k i o -> k (i o)")).then_inc(loaded, 16)
                    sp.dma_start(w3s[:, :], w3).then_inc(loaded, 16)
                    sp.dma_start(w4s[:, :], w4).then_inc(loaded, 16)
                    for n, (b, width) in enumerate(((b1, H1), (b2, H1), (b3, H1), (b4, D))):
                        sp.dma_start(bias[:, n, 0:width], b.partition_broadcast(P)).then_inc(loaded, 16)
                    sp.wait_ge(loaded, 7 * 16)

            linear("l1", lambda t: acc[:, 0, t * (K + 1):t * (K + 1) + K], K, w1s[:, :], H1, h, scale=rdeg)
            bias_elu("e1", h[:, :, :], bias[:, 0, :])
            build_corners("z2", H1, h, w2, corners2)
            spline("s2", H1, corners2)
            with Phase():
                with nc.Block() as block:

                    @block.vector
                    def _(v):
                        v.tensor_tensor(h[:, :, :], acc[:, 0, 0:NT * H1].rearrange("p (t c) -> p t c", t=NT), bcast(rdeg[:, :], 2, H1), ALU.mult)
            bias_elu("e2", h[:, :, :], bias[:, 1, :])
            linear("l3", lambda t: h[:, t, :], H1, w3s[:, :], H1, h)
            bias_elu("e3", h[:, :, :], bias[:, 2, :])
            linear("l4", lambda t: h[:, t, :], H1, w4s[:, :], D, tn[:, 0, :, :])

            QUAD = 4
            own = sb("own4", [P, 2, 2, QUAD, P])
            pick = sb("pick", [P, 2, 2, QUAD * P])
            which = sb("which", [P, 2, 2, QUAD, NT])
            masked = sb("masked", [P, 2, QUAD, D, 2, NT])
            diff = sb("diff", [P, T, D])
            pick_ps = ps("pick_ps", [P, 2, 2, QUAD * P])
            all_ps = ps("all_ps", [P, 2, 2, BANK])
            made, turned, copied, picked, step, taken = (sem(n) for n in ("made4", "turned4", "copied4", "picked4", "step4", "taken4"))
            with nc.Block() as block:

                @block.vector
                def _(v):
                    ch = Chain(v, step)
                    ch.link(v.tensor_tensor(tn[:, 0, :, :], tn[:, 0, :, :], bcast(bias[:, 3, 0:D], 1, NT), ALU.add))
                    ch.link(v.tensor_scalar(tn[:, 1, :, :], tn[:, 0, :, :], -1.0, None, ALU.mult))

                    def make(n, g):
                        v.wait_ge(turned, n + 1)
                        s = bass.ds(n * QUAD, QUAD)
                        for j in range(QUAD):
                            e = bass.ds(n * QUAD + j, 1)
                            v.tensor_scalar(own[:, g, 0, j, :], iota128[:, :], dstlo[:, e], None, ALU.is_equal)
                            last = v.tensor_scalar(own[:, g, 1, j, :], iota128[:, :], srclo[:, e], None, ALU.is_equal)
                        last.then_inc(made, 1)
                        it = bcast(iota128[:, 0:NT], 1, QUAD)
                        v.tensor_tensor(which[:, g, 0, :, :], it, bcast(dsthi[:, s], 2, NT), ALU.is_equal)
                        ch.link(v.tensor_tensor(which[:, g, 1, :, :], it, bcast(bucket[:, s], 2, NT), ALU.is_equal))

                    def take(n, g):
                        v.wait_ge(picked, n + 3)
                        for side in range(2):
                            a = all_ps[:, g, side, 0:QUAD * NT * D].rearrange("p (j b c) -> p j b c", j=QUAD, b=NT)
                            m = masked[:, g, :, :, side, :].rearrange("p j c b -> p j b c")
                            last = v.tensor_tensor(m, a, bcast(which[:, g, side, :, :], 3, D), ALU.mult)
                        ch.link(last)
                        v.tensor_reduce(diff[:, bass.ds(n * QUAD, QUAD), :].rearrange("p t c -> p (t c)"),
                                        masked[:, g, :, :, :, :].rearrange("p j c s b -> p (j c) (s b)"), AX, ALU.add).then_inc(taken, 1)

                    make(0, 0)
                    base = ch.off + ch.k
                    trips = T // (2 * QUAD)
                    with v.Fori(0, trips - 1) as i:
                        ch.off, ch.k = base + i * 4, 0
                        make(2 * i + 1, 1)
                        take(2 * i, 0)
                        make(2 * i + 2, 0)
                        take(2 * i + 1, 1)
                    ch.off, ch.k = base + (trips - 1) * 4, 0
                    make(2 * trips - 1, 1)
                    take(2 * trips - 2, 0)
                    take(2 * trips - 1, 1)
                    v.wait_ge(taken, 2 + 2 * trips)
                    ch.link(v.tensor_tensor(pseudo[:, :, :], pseudo[:, :, :], diff[:, :, :], ALU.add))
                    v.tensor_scalar(pseudo[:, :, :], pseudo[:, :, :], 0.0, 1.0, ALU.max, ALU.min)

                @block.tensor
                def _(pe):
                    pe.sem_inc(turned, 2)

                    def turn(n, g):
                        pe.wait_ge(copied, n + 1)
                        pe.wait_ge(made, n + 1)
                        for side in range(2):
                            for j in range(QUAD):
                                last = pe.transpose(pick_ps[:, g, side, j * P:(j + 1) * P], own[:, g, side, j, :], ident[:, :])
                        last.then_inc(turned, 1)

                    def select(n, g):
                        pe.wait_ge(copied, n + 3)
                        pe.wait_ge(taken, n + 1)
                        for side in range(2):
                            tt = tn[:, side, :, :].rearrange("p t c -> p (t c)")
                            for j in range(QUAD):
                                last = pe.matmul(all_ps[:, g, side, j * NT * D:(j + 1) * NT * D], pick[:, g, side, j * P:(j + 1) * P], tt, start=True, stop=True)
                        last.then_inc(picked, 1)

                    trips = T // (2 * QUAD)
                    turn(0, 0)
                    with pe.Fori(0, trips - 1) as i:
                        turn(2 * i + 1, 1)
                        select(2 * i, 0)
                        turn(2 * i + 2, 0)
                        select(2 * i + 1, 1)
                    turn(2 * trips - 1, 1)
                    select(2 * trips - 2, 0)
                    select(2 * trips - 1, 1)

                @block.scalar
                def _(act):
                    act.sem_inc(copied, 2)
                    act.sem_inc(taken, 2)
                    act.sem_inc(picked, 2)

                    def copy(n, g):
                        act.wait_ge(picked, n + 1)
                        act.wait_ge(turned, n + 3)
                        act.activation(pick[:, g, :, :], pick_ps[:, g, :, :], ACT.Copy).then_inc(copied, 1)

                    with act.Fori(0, T // (2 * QUAD)) as i:
                        copy(2 * i, 0)
                        copy(2 * i + 1, 1)

        def norm_relu(name, u, result):
            with Phase():
                mean = sb(name + "_mean", [P, NT])
                var = sb(name + "_var", [P, NT])
                inv = sb(name + "_inv", [P, NT])
                tmp = sb(name + "_tmp", [P, NT])
                sq = sb(name + "_sq", [P, NT, C])
                step, turn = sem(name + "_step"), sem(name + "_turn")
                with nc.Block() as block:

                    @block.vector
                    def _(v):
                        ch = Chain(v, step)
                        ch.link(v.tensor_reduce(mean[:, :], u, AX, ALU.add))
                        ch.link(v.tensor_scalar(mean[:, :], mean[:, :], 1.0 / C, None, ALU.mult))
                        ch.link(v.tensor_tensor(result, u, bcast(mean[:, :], 2, C), ALU.subtract))
                        ch.link(v.tensor_tensor(sq[:, :, :], result, result, ALU.mult))
                        ch.link(v.tensor_reduce(var[:, :], sq[:, :, :], AX, ALU.add))
                        ch.link(v.tensor_scalar(var[:, :], var[:, :], 1.0 / C, EPS, ALU.mult, ALU.add))
                        v.reciprocal(tmp[:, :], var[:, :]).then_inc(turn, 1)
                        v.wait_ge(turn, 2)
                        refine(v, ch, inv[:, :], var[:, :], tmp[:, :])
                        ch.link(v.tensor_tensor(result, result, bcast(inv[:, :], 2, C), ALU.mult))
                        v.tensor_scalar(result, result, 0.0, None, ALU.max)

                    @block.scalar
                    def _(act):
                        act.wait_ge(turn, 1)
                        act.activation(inv[:, :], tmp[:, :], ACT.Sqrt).then_inc(turn, 1)

        with Phase():
            loaded, step = sem("loaded5"), sem("step5")
            with nc.Block() as block:

                @block.vector
                def _(v):
                    v.memset(xn[:, :, :], 0.0).then_inc(step, 1)

                @block.sync
                def _(sp):
                    sp.wait_ge(step, 1)
                    sp.dma_start(xn[:, 0:NT - 1, :], x[0:(NT - 1) * P, :].rearrange("(t p) c -> p t c", p=P)).then_inc(loaded, 16)
                    sp.dma_start(xn[0:NREST, NT - 1, :], x[(NT - 1) * P:N, :]).then_inc(loaded, 16)
                    sp.wait_ge(loaded, 32)

        with Phase():
            S = 3 * C
            chunks = [(c, min(BANK, N - c)) for c in range(0, N, BANK)]
            cur = sb("cur", [P, NT, C])
            total = sb("total", [P, NT, C])
            part = sb("part", [P, NT, C])
            parts = sb("parts", [P, NT, S], BF16)
            nodes16 = sb("nodes16", [P, NP], I16)
            gidx = sb("gidx", [P, T], I32)
            stage = sb("stage5", [P, 2, HALF], I32)
            gath = sb("gath", [P, 2, HALF, S], BF16)
            RING = 4
            hot = sb("hot", [P, RING, NP], BF16)
            zb = sb("zb5", [P, BANK], BF16)
            flat = sb("flat", [S, NP])
            three = sb("three", [S, C])
            norm_relu("n0", xn[:, :, :], cur[:, :, :])
            with Phase():
                iotas, step = sem("iotas6"), sem("step6")
                with nc.Block() as block:

                    @block.gpsimd
                    def _(pool):
                        pool.iota(nodes16[:, :], [[1, NP]], base=0, channel_multiplier=0).then_inc(iotas, 1)

                    @block.vector
                    def _(v):
                        ch = Chain(v, step)
                        v.memset(zb[:, :], 0.0)
                        v.memset(flat[:, :], 0.0)
                        v.tensor_copy(total[:, :, :], cur[:, :, :])
                        v.tensor_scalar(gidx[:, :], esrc[:, :], 0.0, None, ALU.max)
                        for s in range(3):
                            last = v.tensor_copy(three[s * C:(s + 1) * C, :], ident[s * C:(s + 1) * C, s * C:(s + 1) * C])

            def propagate(layer):
                name = f"p{layer}"
                with Phase():
                    sums_ps = ps(name + "_sums_ps", [S, 7 * BANK])
                    step, split, kept = sem(name + "_step"), sem(name + "_split"), sem(name + "_kept")
                    staged, made, used, gate, done, moved = (sem(name + n) for n in ("_staged", "_made", "_used", "_gate", "_done", "_moved"))
                    fetched = [sem(f"{name}_fetched{g}") for g in range(2)]
                    with nc.Block() as block:

                        @block.sync
                        def _(sp):
                            sp.wait_ge(split, 1)
                            sp.dma_start(ytab.rearrange("(t p) c -> p t c", p=P), parts[:, :, :]).then_inc(kept, 16)

                        @block.gpsimd
                        def _(pool):
                            pool.wait_ge(kept, 16)
                            with pool.Fori(0, TRIPS) as i:
                                for g in range(2):
                                    pool.wait_ge(staged, 2 * i + g + 1)
                                    pool.sem_inc(gate, 1)
                                    for j in range(HALF):
                                        pool.indirect_dma_start(gath[:, g, j, :], None, ytab,
                                                                bass.IndirectOffsetOnAxis(ap=stage[:, g, j:j + 1], axis=0)).then_inc(fetched[g], 16)

                        @block.vector
                        def _(v):
                            ch = Chain(v, step)
                            ch.link(v.tensor_tensor(cur[:, :, :], cur[:, :, :], bcast(dis[:, :], 2, C), ALU.mult))
                            for s in range(3):
                                ch.link(v.tensor_copy(parts[:, :, s * C:(s + 1) * C], cur[:, :, :]))
                                if s < 2:
                                    ch.link(v.tensor_copy(part[:, :, :], parts[:, :, s * C:(s + 1) * C]))
                                    ch.link(v.tensor_tensor(cur[:, :, :], cur[:, :, :], part[:, :, :], ALU.subtract))
                            v.sem_inc(split, 1)

                            def put(n, g):
                                v.tensor_copy(stage[:, g, :], gidx[:, bass.ds(n * HALF, HALF)]).then_inc(staged, 1)

                            def make(n, g):
                                for j in range(HALF):
                                    v.wait_ge(used, n * HALF + (j + 1))
                                    v.tensor_scalar(hot[:, j % RING, 0:N], nodes16[:, 0:N], edst[:, bass.ds(n * HALF + j, 1)], None, ALU.is_equal).then_inc(made, 1)

                            put(0, 0)
                            put(1, 1)
                            with v.Fori(0, TRIPS - 1) as i:
                                for g in range(2):
                                    make(2 * i + g, g)
                                    v.wait_ge(used, (2 * i + g + 1) * HALF + RING)
                                    put(2 * i + g + 2, g)
                            for g in range(2):
                                make(2 * TRIPS - 2 + g, g)

                        @block.tensor
                        def _(pe):
                            for c, w in chunks:
                                pe.matmul(sums_ps[:, c:c + w], zb[:, 0:S], zb[:, 0:w], start=True, stop=False)
                            pe.sem_inc(used, RING)
                            with pe.Fori(0, TRIPS) as i:
                                for g in range(2):
                                    pe.wait_ge(fetched[g], (i + 1) * (HALF * 16))
                                    for j in range(HALF):
                                        pe.wait_ge(made, i * BODY + (g * HALF + j + 1))
                                        for c, w in chunks:
                                            last = pe.matmul(sums_ps[:, c:c + w], gath[:, g, j, :], hot[:, j % RING, c:c + w], start=False, stop=False)
                                        last.then_inc(used, 1)
                            for c, w in chunks:
                                last = pe.matmul(sums_ps[:, c:c + w], zb[:, 0:S], zb[:, 0:w], start=False, stop=True)
                            last.then_inc(done, 1)

                        @block.scalar
                        def _(act):
                            act.wait_ge(done, 1)
                            act.activation(flat[:, 0:N], sums_ps[:, 0:N], ACT.Copy)

                with Phase():
                    node_ps = ps(name + "_node_ps", [P, NT * C])
                    turned, step = sem(name + "_turned"), sem(name + "_step2")
                    with nc.Block() as block:

                        @block.tensor
                        def _(pe):
                            for t in range(NT):
                                last = pe.matmul(node_ps[:, t * C:(t + 1) * C], flat[:, t * P:(t + 1) * P], three[:, :], start=True, stop=True)
                            last.then_inc(turned, 1)

                        @block.vector
                        def _(v):
                            ch = Chain(v, step)
                            v.wait_ge(turned, 1)
                            ch.link(v.tensor_tensor(cur[:, :, :], node_ps[:, :].rearrange("p (t c) -> p t c", t=NT), bcast(dis[:, :], 2, C), ALU.mult))
                            ch.link(v.tensor_tensor(total[:, :, :], total[:, :, :], cur[:, :, :], ALU.add))
                            if layer == LAYERS - 1:
                                ch.link(v.tensor_scalar(total[:, :, :], total[:, :, :], 1.0 / (LAYERS + 1), None, ALU.mult))
                                v.tensor_tensor(xn[:, :, :], xn[:, :, :], total[:, :, :], ALU.add)

            for layer in range(LAYERS):
                propagate(layer)

        norm_relu("n1", xn[:, :, :], h[:, :, 0:C])
        build_corners("z3", C, h, wc, corners3)
        spline("s3", C, corners3)
        with Phase():
            bias3 = sb("bias3", [P, C])
            loaded, step, ready = sem("loaded7"), sem("step7"), sem("ready7")
            with nc.Block() as block:

                @block.vector
                def _(v):
                    ch = Chain(v, step)
                    r = acc[:, 0, 0:NT * C].rearrange("p (t c) -> p t c", t=NT)
                    ch.link(v.tensor_tensor(r, r, bcast(rdeg[:, :], 2, C), ALU.mult))
                    v.wait_ge(loaded, 16)
                    ch.link(v.tensor_tensor(r, r, bcast(bias3[:, :], 1, NT), ALU.add))
                    v.tensor_tensor(xn[:, :, :], xn[:, :, :], r, ALU.add).then_inc(ready, 1)

                @block.sync
                def _(sp):
                    sp.dma_start(bias3[:, :], bc.partition_broadcast(P)).then_inc(loaded, 16)
                    sp.wait_ge(ready, 1)
                    sp.dma_start(out[0:(NT - 1) * P, :].rearrange("(t p) c -> p t c", p=P), xn[:, 0:NT - 1, :]).then_inc(loaded, 16)
                    sp.dma_start(out[(NT - 1) * P:N, :], xn[0:NREST, NT - 1, :]).then_inc(loaded, 16)
                    sp.wait_ge(loaded, 48)


_INS = ['x', 'src', 'dst', 'edge_attr_3', 'L1_gnn_stn1_w', 'L1_gnn_stn1_b', 'L1_gnn_stn2_w', 'L1_gnn_stn2_b',
        'L1_gnn_stn3_w', 'L1_gnn_stn3_b', 'L1_gnn_stn4_w', 'L1_gnn_stn4_b', 'L1_gnn_conv_w', 'L1_gnn_conv_b']
_OUTS = [((N, C), 'float32')]


def kernel(**inputs):
    import numpy as _np
    import concourse.bacc as _bacc
    from concourse import mybir as _mybir
    from concourse.bass_utils import run_bass_kernel_spmd as _run

    nc = _bacc.Bacc("TRN2", target_bir_lowering=False, num_devices=1)
    arrays, args = {}, []
    for name in _INS:
        a = _np.ascontiguousarray(inputs[name])
        arrays[f"in_{name}_dram"] = a
        args.append(nc.dram_tensor(f"in_{name}_dram", a.shape, _mybir.dt.from_np(a.dtype), kind="ExternalInput").ap())
    for i, (shape, dtype) in enumerate(_OUTS):
        dt = _mybir.dt.from_np(_np.dtype(dtype))
        args.append(nc.dram_tensor(f"out_{i}_dram", shape, dt, kind="ExternalOutput").ap())
    gnn(nc, *args)
    r = _run(nc, [arrays], core_ids=[0])
    got = tuple(r.results[0][f"out_{i}_dram"] for i in range(len(_OUTS)))
    return got[0]
```

```python
from contextlib import ExitStack

import concourse.bass as bass
from concourse import mybir

F32 = mybir.dt.float32
BF16 = mybir.dt.bfloat16
I32 = mybir.dt.int32
I16 = mybir.dt.int16
ALU = mybir.AluOpType
ACT = mybir.ActivationFunctionType
AX = mybir.AxisListType.X

P = 128
N = 3125
NT = -(-N // P)
NP = NT * P
NREST = N - (NT - 1) * P
E = 100000
EP = 125
EC = E // EP
HALF = 8
BODY = 2 * HALF
T = -(-(E // P + NT) // BODY) * BODY
TRIPS = T // BODY
D = 3
KS = 5
K = KS ** D
C = 32
H1 = 64
LAYERS = 3
REC = 8
DREC = 2
CELLS = 4 * KS * 4
BANK = 512
EPS = 1e-5


class Chain:

    def __init__(self, eng, sem):
        self.eng, self.sem, self.base, self.off, self.k = eng, sem, 0, 0, 0

    def link(self, ins):
        ins.then_inc(self.sem, 1)
        self.k += 1
        self.eng.wait_ge(self.sem, self.off + self.k)


def bcast(ap, dim, n):
    v = ap.unsqueeze(dim)
    shape = list(v.shape)
    shape[dim] = n
    return v.broadcast_to(shape)


def gnn(nc, x, src, dst, edge_attr_3, w1, b1, w2, b2, w3, b3, w4, b4, wc, bc, out):
    recs = nc.dram_tensor("recs", (P * T, REC), F32, kind="Internal").ap()
    corners2 = nc.dram_tensor("corners2", (NP * CELLS, 4 * H1), F32, kind="Internal").ap()
    corners3 = nc.dram_tensor("corners3", (NP * CELLS, 4 * C), F32, kind="Internal").ap()
    drecs = nc.dram_tensor("drecs", (P * T, DREC), F32, kind="Internal").ap()
    ytab = nc.dram_tensor("ytab", (NP, C), F32, kind="Internal").ap()

    with ExitStack() as whole:
        scopes = [whole]

        def sb(name, shape, dt=F32):
            return scopes[-1].enter_context(nc.sbuf_tensor(name, shape, dt))

        def ps(name, shape, dt=F32):
            return scopes[-1].enter_context(nc.psum_tensor(name, shape, dt))

        def sem(name):
            return scopes[-1].enter_context(nc.semaphore(name))

        class Phase:

            def __enter__(self):
                scopes.append(ExitStack())
                scopes[-1].__enter__()

            def __exit__(self, *a):
                scopes.pop().__exit__(*a)

        iota128 = sb("iota128", [P, P])
        pidx = sb("pidx", [P, 1])
        ident = sb("ident", [P, P])
        ones = sb("ones", [P, P])
        zeros = sb("zeros", [P, BANK], BF16)
        bucket = sb("bucket", [P, T], I32)
        srclo = sb("srclo", [P, T])
        edst = sb("edst", [P, T])
        dstlo = sb("dstlo", [P, T])
        dsthi = sb("dsthi", [P, T])
        pseudo = sb("pseudo", [P, T, D])
        dbucket = sb("dbucket", [P, T], I32)
        dback = sb("dback", [P, T, DREC])
        gsrc = sb("gsrc", [P, T], I32)
        dlow = sb("dlow", [P, T], I32)
        dposi = sb("dposi", [EP, EC], I32)
        drec = sb("drec", [EP, EC, DREC])
        rdeg = sb("rdeg", [P, NT])
        dis = sb("dis", [P, NT])
        xn = sb("xn", [P, NT, C])
        h = sb("h", [P, NT, H1])

        def scatter(name, posi, rec, width, recs):
            stage_i = sb(name + "_stage_i", [EP, BODY], I32)
            stage_r = sb(name + "_stage_r", [EP, BODY, width])
            staged, gate, gate_p = sem(name + "_staged"), sem(name + "_gate"), sem(name + "_gate_p")
            stored = [sem(f"{name}_stored{g}") for g in range(2)]
            turns = EC // BODY

            def stage(act):
                def put(turn, g):
                    act.activation(stage_i[:, g * HALF:(g + 1) * HALF], posi[:, bass.ds(turn * BODY + g * HALF, HALF)], ACT.Copy)
                    act.activation(stage_r[:, g * HALF:(g + 1) * HALF, :], rec[:, bass.ds(turn * BODY + g * HALF, HALF), :], ACT.Copy).then_inc(staged, 1)

                put(0, 0)
                put(0, 1)
                with act.Fori(0, turns - 1) as i:
                    for g in range(2):
                        act.wait_ge(stored[g], (i + 1) * (16 * HALF))
                        act.sem_inc(gate, 1)
                        put(i + 1, g)

            def store(pool):
                with pool.Fori(0, turns) as i:
                    for g in range(2):
                        pool.wait_ge(staged, 2 * i + g + 1)
                        pool.sem_inc(gate_p, 1)
                        for j in range(g * HALF, (g + 1) * HALF):
                            pool.indirect_dma_start(recs, bass.IndirectOffsetOnAxis(ap=stage_i[:, j:j + 1], axis=0),
                                                    stage_r[:, j, :], None).then_inc(stored[g], 16)
                for g in range(2):
                    pool.wait_ge(stored[g], turns * HALF * 16)

            return stage, store

        with Phase():
            esi = sb("esi", [EP, EC], I32)
            edi = sb("edi", [EP, EC], I32)
            eps_in = sb("eps_in", [EP, EC, D])
            hi_i = sb("hi_i", [EP, EC], I32)
            key = sb("key", [EP, EC])
            eq = sb("eq", [EP, 2, EC])
            cum = sb("cum", [EP, 2, EC])
            zero = sb("zero", [EP, EC])
            mine = sb("mine", [EP, 2, EC])
            pos = sb("pos", [EP, EC])
            posi = sb("posi", [EP, EC], I32)
            low_i = sb("low_i", [EP, EC], I32)
            high_i = sb("high_i", [EP, EC], I32)
            posf = sb("posf", [EP, EC])
            rec = sb("rec", [EP, EC, REC])
            pad = sb("pad", [P, T, REC])
            dpad = sb("dpad", [P, T, DREC])
            tot = sb("tot", [EP, 2, NT])
            tri = sb("tri", [P, P])
            cnti = sb("cnti", [P, NT], I32)
            tiles = sb("tiles", [P, NT])
            tend = sb("tend", [P, NT])
            tstart = sb("tstart", [P, NT])
            off = sb("off", [EP, NT])
            iotat = sb("iotat", [P, T])
            bf = sb("bf", [P, 2, T])
            count_ps = ps("count_ps", [P, 2, 2, BANK])
            loaded, iotas, step, tot_ready, counts = (sem(n) for n in ("loaded", "iotas", "step", "tot_ready", "counts"))
            padded, pad_ready, ranked = (sem(n) for n in ("padded", "pad_ready", "ranked"))
            stage_src, store_src = scatter("by_src", posi, rec, REC, recs)
            with nc.Block() as block:

                @block.sync
                def _(sp):
                    sp.dma_start(esi[:, :], src.rearrange("(p c) -> p c", p=EP)).then_inc(loaded, 16)
                    sp.dma_start(edi[:, :], dst.rearrange("(p c) -> p c", p=EP)).then_inc(loaded, 16)
                    sp.dma_start(eps_in[:, :, :], edge_attr_3.rearrange("(p c) d -> p c d", p=EP)).then_inc(loaded, 16)
                    sp.wait_ge(pad_ready, 1)
                    sp.dma_start(recs.rearrange("(p t) r -> p (t r)", p=P), pad[:, :, :].rearrange("p t r -> p (t r)")).then_inc(padded, 16)
                    sp.dma_start(drecs.rearrange("(p t) r -> p (t r)", p=P), dpad[:, :, :].rearrange("p t r -> p (t r)")).then_inc(padded, 16)

                @block.tensor
                def _(pe):
                    for k in range(2):
                        pe.wait_ge(tot_ready, k + 1)
                        nc.tensor.matmul(count_ps[0:EP, k, 0, 0:NT], tri[0:EP, 0:EP], tot[:, k, :], start=True, stop=True)
                        nc.tensor.matmul(count_ps[:, k, 1, 0:NT], ones[0:EP, :], tot[:, k, :], start=True, stop=True).then_inc(counts, 1)

                @block.scalar
                def _(act):
                    act.wait_ge(ranked, 1)
                    stage_src(act)

                @block.gpsimd
                def _(pool):
                    pool.iota(iota128[:, :], [[1, P]], base=0, channel_multiplier=0, allow_small_or_imprecise_dtypes=True).then_inc(iotas, 1)
                    pool.iota(pidx[:, :], [[0, 1]], base=0, channel_multiplier=1, allow_small_or_imprecise_dtypes=True).then_inc(iotas, 1)
                    pool.iota(iotat[:, :], [[1, T]], base=0, channel_multiplier=0, allow_small_or_imprecise_dtypes=True).then_inc(iotas, 1)
                    pool.wait_ge(padded, 32)
                    store_src(pool)

                @block.vector
                def _(v):
                    ch = Chain(v, step)

                    def rank(k, node, row, bucket_of):
                        ch.link(v.tensor_scalar(hi_i[:, :], node[:, :], 7, None, ALU.arith_shift_right))
                        ch.link(v.tensor_copy(key[:, :], hi_i[:, :]))
                        for b in range(NT):
                            last = v.tensor_scalar(eq[:, b % 2, :], key[:, :], float(b), None, ALU.is_equal, ALU.add, accum_out=tot[:, k, b:b + 1])
                            ch.link(last)
                        v.memset(pos[:, :], 0.0)
                        v.memset(bf[:, 1, :], -1.0).then_inc(tot_ready, 1)
                        v.wait_ge(counts, k + 1)
                        ch.link(v.tensor_scalar(cnti[:, :], count_ps[:, k, 1, 0:NT], float(P - 1), None, ALU.add))
                        ch.link(v.tensor_scalar(cnti[:, :], cnti[:, :], 7, None, ALU.arith_shift_right))
                        ch.link(v.tensor_copy(tiles[:, :], cnti[:, :]))
                        ch.link(v.tensor_tensor_scan(tend[:, :], ones[:, 0:NT], tiles[:, :], 0.0, ALU.mult, ALU.add))
                        ch.link(v.tensor_tensor(tstart[:, :], tend[:, :], tiles[:, :], ALU.subtract))
                        ch.link(v.tensor_scalar(off[:, :], tstart[0:EP, :], float(P), -1.0, ALU.mult, ALU.add))
                        ch.link(v.tensor_tensor(off[:, :], count_ps[0:EP, k, 0, 0:NT], off[:, :], ALU.add))
                        for b in range(NT):
                            q = b % 2
                            ch.link(v.tensor_scalar(eq[:, q, :], key[:, :], float(b), None, ALU.is_equal))
                            ch.link(v.tensor_tensor_scan(cum[:, q, :], eq[:, q, :], zero[:, :], 0.0, ALU.add, ALU.add))
                            ch.link(v.scalar_tensor_tensor(mine[:, q, :], cum[:, q, :], off[:, b:b + 1], eq[:, q, :], ALU.add, ALU.mult))
                            ch.link(v.tensor_tensor(pos[:, :], pos[:, :], mine[:, q, :], ALU.add))
                        ch.link(v.tensor_copy(low_i[:, :], pos[:, :]))
                        ch.link(v.tensor_scalar(high_i[:, :], low_i[:, :], 7, None, ALU.arith_shift_right))
                        ch.link(v.tensor_scalar(low_i[:, :], low_i[:, :], P - 1, None, ALU.bitwise_and))
                        v.tensor_copy(posf[:, :], low_i[:, :])
                        ch.link(v.tensor_copy(mine[:, 0, :], high_i[:, :]))
                        ch.link(v.scalar_tensor_tensor(pos[:, :], posf[:, :], float(T), mine[:, 0, :], ALU.mult, ALU.add))
                        v.tensor_copy(row[:, :], pos[:, :]).then_inc(ranked, 1)
                        for b in range(NT):
                            ch.link(v.scalar_tensor_tensor(bf[:, b % 2, :], iotat[:, :], tstart[:, b:b + 1], bf[:, (b + 1) % 2, :], ALU.is_ge, ALU.add))
                        ch.link(v.tensor_copy(bucket_of[:, :], bf[:, (NT - 1) % 2, :]))

                    ch.link(v.memset(pad[:, :, :], 0.0))
                    v.memset(dpad[:, :, :], -1.0)
                    v.memset(pad[:, :, 0:2], -1.0).then_inc(pad_ready, 1)
                    v.memset(ones[:, :], 1.0)
                    v.memset(zero[:, :], 0.0)
                    v.memset(zeros[:, :], 0.0)
                    ch.link(v.memset(rec[:, :, :], 0.0))
                    v.wait_ge(iotas, 3)
                    v.tensor_scalar(ident[:, :], iota128[:, :], pidx[:, 0:1], None, ALU.is_equal)
                    v.tensor_scalar(tri[:, :], iota128[:, :], pidx[:, 0:1], None, ALU.is_gt)
                    v.wait_ge(loaded, 48)
                    for k, e in enumerate((esi, edi)):
                        v.tensor_copy(rec[:, :, k], e[:, :])
                        v.tensor_copy(drec[:, :, k], e[:, :])
                    v.tensor_copy(rec[:, :, 2:2 + D], eps_in[:, :, :])
                    rank(0, esi, posi, bucket)
                    rank(1, edi, dposi, dbucket)

        def corner_tables(v, ch, i0, fr, fr0, weight, cidx, tmp):
            ch.link(v.tensor_scalar(fr[:, :, :], pseudo[:, :, :], float(KS - 1), None, ALU.mult))
            ch.link(v.tensor_scalar(i0[:, :, :], fr[:, :, :], 1.0, None, ALU.is_ge))
            for knot in range(2, KS - 1):
                ch.link(v.scalar_tensor_tensor(i0[:, :, :], fr[:, :, :], float(knot), i0[:, :, :], ALU.is_ge, ALU.add))
            ch.link(v.tensor_tensor(fr[:, :, :], fr[:, :, :], i0[:, :, :], ALU.subtract))
            ch.link(v.tensor_scalar(fr0[:, :, :], fr[:, :, :], -1.0, 1.0, ALU.mult, ALU.add))
            w = weight[:, :, :].rearrange("p t (y x z) -> p t y x z", y=2, x=2)
            side = (fr0, fr)
            for cy in range(2):
                for cx in range(2):
                    v.tensor_tensor(w[:, :, cy, cx, 1], side[cx][:, :, 0], side[cy][:, :, 1], ALU.mult)
            for cy in range(2):
                for cx in range(2):
                    last = v.tensor_tensor(w[:, :, cy, cx, 0], side[cx][:, :, 0], side[cy][:, :, 1], ALU.mult)
            ch.link(last)
            for cz in range(2):
                for c in range(4):
                    cc = w[:, :, c // 2, c % 2, cz]
                    last = v.tensor_tensor(cc, cc, side[cz][:, :, 2], ALU.mult)
            ch.link(last)
            ch.link(v.tensor_scalar(tmp[:, :], edst[:, :], 0.0, float(CELLS), ALU.max, ALU.mult))
            for d, stride in ((0, KS * 4), (1, 4), (2, 1)):
                ch.link(v.scalar_tensor_tensor(tmp[:, :], i0[:, :, d], float(stride), tmp[:, :], ALU.mult, ALU.add))
            v.tensor_copy(cidx[:, :, 0], tmp[:, :])
            ch.link(v.tensor_scalar(cidx[:, :, 1], tmp[:, :], 4.0, None, ALU.add))

        def refine(v, ch, s, a, tmp):
            ch.link(v.tensor_tensor(tmp, s, s, ALU.mult))
            ch.link(v.tensor_tensor(tmp, tmp, a, ALU.mult))
            ch.link(v.tensor_scalar(tmp, tmp, -0.5, 1.5, ALU.mult, ALU.add))
            ch.link(v.tensor_tensor(s, s, tmp, ALU.mult))

        def clear(pe, sums, columns):
            for c in range(0, columns, BANK):
                pe.matmul(sums[:, c:min(c + BANK, columns)], zeros[:, 0:P], zeros[:, 0:min(BANK, columns - c)], start=True, stop=False)

        def close(pe, sums, columns):
            for c in range(0, columns, BANK):
                last = pe.matmul(sums[:, c:min(c + BANK, columns)], zeros[:, 0:P], zeros[:, 0:min(BANK, columns - c)], start=False, stop=True)
            return last

        def linear(name, tile_of, kin, w, kout, result, scale=None):
            G = 5
            with Phase():
                turned = sb(name + "_turned", [kin, G * P])
                turned_ps = ps(name + "_turned_ps", [P, 2 * BANK])
                out_ps = ps(name + "_out_ps", [P, BANK])
                in_psum, in_sbuf, multiplied, kept = (sem(name + x) for x in ("_t", "_s", "_m", "_k"))
                with nc.Block() as block:

                    @block.tensor
                    def _(pe):
                        for i in range(NT // G):
                            for j in range(G):
                                last = pe.transpose(turned_ps[0:kin, j * P:(j + 1) * P], tile_of(i * G + j), ident[:, :])
                            last.then_inc(in_psum, 1)
                            pe.wait_ge(in_sbuf, i + 1)
                            pe.wait_ge(kept, i + 1)
                            for j in range(G):
                                last = pe.matmul(out_ps[:, j * kout:(j + 1) * kout], turned[:, j * P:(j + 1) * P], w, start=True, stop=True)
                            last.then_inc(multiplied, 1)

                    @block.scalar
                    def _(act):
                        with act.Fori(0, NT // G) as i:
                            act.wait_ge(in_psum, i + 1)
                            act.activation(turned[:, :], turned_ps[0:kin, 0:G * P], ACT.Copy).then_inc(in_sbuf, 1)

                    @block.vector
                    def _(v):
                        v.sem_inc(kept, 1)
                        with v.Fori(0, NT // G) as i:
                            v.wait_ge(multiplied, i + 1)
                            r = result[:, bass.ds(i * G, G), :]
                            o = out_ps[:, 0:G * kout].rearrange("p (t c) -> p t c", t=G)
                            if scale is None:
                                v.tensor_copy(r, o).then_inc(kept, 1)
                            else:
                                v.tensor_tensor(r, o, bcast(scale[:, bass.ds(i * G, G)], 2, kout), ALU.mult).then_inc(kept, 1)

        def bias_elu(name, u, bias):
            with Phase():
                low = sb(name + "_low", [P, NT, H1])
                step, cut, raised = sem(name + "_step"), sem(name + "_cut"), sem(name + "_raised")
                with nc.Block() as block:

                    @block.vector
                    def _(v):
                        ch = Chain(v, step)
                        ch.link(v.tensor_tensor(u, u, bcast(bias, 1, NT), ALU.add))
                        v.tensor_scalar(low[:, :, :], u, 0.0, None, ALU.min).then_inc(cut, 1)
                        v.wait_ge(raised, 1)
                        ch.link(v.tensor_scalar(u, u, 0.0, -1.0, ALU.max, ALU.add))
                        v.tensor_tensor(u, u, low[:, :, :], ALU.add)

                    @block.scalar
                    def _(act):
                        act.wait_ge(cut, 1)
                        act.activation(low[:, :, :], low[:, :, :], ACT.Exp).then_inc(raised, 1)

        def build_corners(name, f, nodes, w_dram, table):
            G = 5
            plane = KS * KS * f
            banks = -(-plane // BANK)
            with Phase():
                w = sb(name + "_w", [f, K * f])
                turned = sb(name + "_turned", [f, NT * P])
                with Phase():
                    turned_ps = ps(name + "_turned_ps", [P, 2, 2 * BANK])
                    in_psum, in_sbuf, loaded = (sem(name + x) for x in ("_t", "_s", "_l"))
                    with nc.Block() as block:

                        @block.sync
                        def _(sp):
                            sp.dma_start(w[:, :].rearrange("i (k o) -> i k o", k=K), w_dram.rearrange("k i o -> i k o")).then_inc(loaded, 16)
                            sp.wait_ge(loaded, 16)

                        @block.tensor
                        def _(pe):
                            for i in range(NT // G):
                                if i >= 2:
                                    pe.wait_ge(in_sbuf, i - 1)
                                for j in range(G):
                                    last = pe.transpose(turned_ps[0:f, i % 2, j * P:(j + 1) * P], nodes[:, i * G + j, 0:f], ident[:, :])
                                last.then_inc(in_psum, 1)

                        @block.scalar
                        def _(act):
                            for i in range(NT // G):
                                act.wait_ge(in_psum, i + 1)
                                act.activation(turned[:, i * G * P:(i + 1) * G * P], turned_ps[0:f, i % 2, 0:G * P], ACT.Copy).then_inc(in_sbuf, 1)

                mine = sb(name + "_mine", [f, P])
                placed, gate_p = sem(name + "_placed"), sem(name + "_gate_p")
                cube = sb(name + "_cube", [P, 4, KS, 4, 2, 2 * f])
                plane_ps = ps(name + "_plane_ps", [P, 2, banks * BANK])
                planes, by_act, by_dve = (sem(name + x) for x in ("_planes", "_by_act", "_by_dve"))
                stored = [sem(f"{name}_stored{i}") for i in range(4)]
                rows = table.rearrange("(t p x r) c -> t p x (r c)", t=NT, p=P, x=4)

                def spread(copy, kx, x, cx):
                    knots = plane_ps[:, kx % 2, 0:plane].rearrange("p (y z o) -> p y z o", y=KS, z=KS)
                    for cz in range(2):
                        last = copy(cube[:, x, :, :, cx, cz * f:(cz + 1) * f], knots[:, :, cz:cz + 4, :])
                    return last

                with nc.Block() as block:

                    @block.gpsimd
                    def _(pool):
                        pool.tensor_copy(mine[:, :], turned[:, 0:P]).then_inc(placed, 1)
                        with pool.Fori(1, NT) as i:
                            pool.wait_ge(planes, i * KS)
                            pool.sem_inc(gate_p, 1)
                            pool.tensor_copy(mine[:, :], turned[:, bass.ds(i * P, P)]).then_inc(placed, 1)

                    @block.tensor
                    def _(pe):
                        with pe.Fori(0, NT) as i:
                            pe.wait_ge(placed, i + 1)
                            for kx in range(KS):
                                if kx == 0:
                                    pe.wait_ge(by_dve, 4 * i + 1)
                                else:
                                    pe.wait_ge(by_act, 4 * i + kx)
                                for c in range(banks):
                                    n = min(BANK, plane - c * BANK)
                                    last = pe.matmul(plane_ps[:, kx % 2, c * BANK:c * BANK + n], mine[:, :],
                                                     w[:, kx * plane + c * BANK:kx * plane + c * BANK + n], start=True, stop=True)
                                last.then_inc(planes, 1)

                    def near(act, i, first):
                        for kx in range(4):
                            if not first:
                                act.wait_ge(stored[kx], i * 16)
                                act.wait_ge(by_dve, 4 * i + kx - 2)
                            act.wait_ge(planes, KS * i + kx + 1)
                            if not first:
                                act.sem_inc(gate_a, 1)
                            spread(lambda o, s: act.activation(o, s, ACT.Copy), kx, kx, 0).then_inc(by_act, 1)

                    def far(v, i, first):
                        for kx in range(1, KS):
                            if not first:
                                v.wait_ge(stored[kx - 1], i * 16)
                            if kx < 4:
                                v.wait_ge(by_act, 4 * i + kx + 2)
                                v.tensor_copy(cube[:, kx - 1, :, :, 1, :], cube[:, kx, :, :, 0, :]).then_inc(by_dve, 1)
                            else:
                                v.wait_ge(planes, KS * i + kx + 1)
                                spread(v.tensor_copy, kx, kx - 1, 1).then_inc(by_dve, 1)

                    gate_a = sem(name + "_gate_a")

                    @block.scalar
                    def _(act):
                        act.sem_inc(by_act, 1)
                        near(act, 0, True)
                        with act.Fori(1, NT) as i:
                            near(act, i, False)

                    @block.vector
                    def _(v):
                        v.sem_inc(by_dve, 1)
                        far(v, 0, True)
                        with v.Fori(1, NT) as i:
                            far(v, i, False)

                    @block.sync
                    def _(sp):
                        with sp.Fori(0, NT) as i:
                            for x in range(4):
                                sp.wait_ge(by_act, 4 * i + x + 2)
                                sp.wait_ge(by_dve, 4 * i + x + 2)
                                sp.dma_start(rows[i, :, x, :], cube[:, x, :, :, :, :].rearrange("p y z a b -> p (y z a b)")).then_inc(stored[x], 16)
                        for x in range(4):
                            sp.wait_ge(stored[x], 16 * NT)

        def spline(name, f, table, result):
            with Phase():
                weight = sb(name + "_weight", [P, T, 8])
                cidx = sb(name + "_cidx", [P, T, 2], I32)
                with Phase():
                    i0 = sb(name + "_i0", [P, T, D])
                    fr = sb(name + "_fr", [P, T, D])
                    fr0 = sb(name + "_fr0", [P, T, D])
                    tmp = sb(name + "_tmp", [P, T])
                    step = sem(name + "_step")
                    with nc.Block() as block:

                        @block.vector
                        def _(v):
                            corner_tables(v, Chain(v, step), i0, fr, fr0, weight, cidx, tmp)

                stage = sb(name + "_stage", [P, 2, HALF * 2], I32)
                rows = sb(name + "_rows", [P, 2, HALF, 2, 4 * f])
                parts = sb(name + "_parts", [P, 2, HALF, 8, f])
                own = sb(name + "_own", [P, 2, HALF, P])
                sums_ps = ps(name + "_sums_ps", [P, NT * f])
                staged, weighted, made, used, gate, gate_a, summed = (sem(name + x) for x in ("_staged", "_weighted", "_made", "_used", "_gate", "_gate_a", "_summed"))
                fetched = [sem(f"{name}_fetched{g}") for g in range(2)]
                with nc.Block() as block:

                    @block.gpsimd
                    def _(pool):
                        with pool.Fori(0, TRIPS) as i:
                            for g in range(2):
                                pool.wait_ge(staged, 2 * i + g + 1)
                                pool.sem_inc(gate, 1)
                                for j in range(HALF):
                                    for c in range(2):
                                        pool.indirect_dma_start(rows[:, g, j, c, :], None, table,
                                                                bass.IndirectOffsetOnAxis(ap=stage[:, g, 2 * j + c:2 * j + c + 1], axis=0)).then_inc(fetched[g], 16)

                    @block.scalar
                    def _(act):
                        def put(n, g):
                            act.activation(stage[:, g, :], cidx[:, bass.ds(n * HALF, HALF), :].rearrange("p t c -> p (t c)"), ACT.Copy).then_inc(staged, 1)

                        put(0, 0)
                        put(1, 1)
                        with act.Fori(0, TRIPS - 1) as i:
                            for g in range(2):
                                act.wait_ge(fetched[g], (i + 1) * (2 * HALF * 16))
                                act.wait_ge(weighted, 2 * i + g + 1)
                                act.sem_inc(gate_a, 1)
                                put(2 * i + g + 2, g)

                    @block.vector
                    def _(v):
                        with v.Fori(0, TRIPS) as i:
                            for g in range(2):
                                n = 2 * i + g
                                s = bass.ds(n * HALF, HALF)
                                v.wait_ge(used, n + 1)
                                v.tensor_tensor(own[:, g, :, :], bcast(iota128[:, :], 1, HALF), bcast(srclo[:, s], 2, P), ALU.is_equal).then_inc(made, 1)
                                v.wait_ge(fetched[g], (i + 1) * (2 * HALF * 16))
                                v.tensor_tensor(parts[:, g, :, :, :].rearrange("p t s o -> p (t s) o"),
                                                rows[:, g, :, :, :].rearrange("p t y (s o) -> p (t y s) o", s=4),
                                                bcast(weight[:, s, :].rearrange("p t s -> p (t s)"), 2, f), ALU.mult).then_inc(weighted, 1)
                        v.wait_ge(summed, 1)
                        v.tensor_tensor(result, sums_ps[:, :].rearrange("p (t o) -> p t o", t=NT), bcast(rdeg[:, :], 2, f), ALU.mult)

                    @block.tensor
                    def _(pe):
                        clear(pe, sums_ps, NT * f)
                        pe.sem_inc(used, 2)
                        with pe.Fori(0, TRIPS) as i:
                            for g in range(2):
                                n = 2 * i + g
                                pe.wait_ge(made, n + 1)
                                pe.wait_ge(weighted, n + 1)
                                for j in range(HALF):
                                    b = pe.value_load(bucket[0:1, bass.ds(n * HALF + j, 1)], min_val=0, max_val=NT - 1)
                                    for c in range(8):
                                        last = pe.matmul(sums_ps[:, bass.ds(b * f, f)], own[:, g, j, :], parts[:, g, j, c, :],
                                                         start=False, stop=False, skip_group_check=True)
                                last.then_inc(used, 1)
                        close(pe, sums_ps, NT * f).then_inc(summed, 1)

        with Phase():
            sums = sb("sums", [P, NT, K + 1])
            w1s = sb("w1s", [K, H1])
            w3s = sb("w3s", [H1, H1])
            w4s = sb("w4s", [H1, D])
            bias = sb("bias", [P, 4, H1])
            tn = sb("tn", [P, 2, NT, D])
            with Phase():
                hat = sb("hat", [P, T, D, KS])
                deg = sb("deg", [P, NT])
                rec_deg = sb("rec_deg", [P, NT])
                nt_tmp = sb("nt_tmp", [P, NT])
                has = sb("has", [P, NT])
                with Phase():
                    back = sb("back", [P, T, REC])
                    ti = sb("ti", [P, T], I32)
                    t2 = sb("t2", [P, T], I32)
                    loaded, step = sem("loaded2"), sem("step2")
                    with nc.Block() as block:

                        @block.sync
                        def _(sp):
                            sp.dma_start(back[:, :, :].rearrange("p t r -> p (t r)"), recs.rearrange("(p t) r -> p (t r)", p=P)).then_inc(loaded, 16)

                        @block.vector
                        def _(v):
                            ch = Chain(v, step)
                            v.wait_ge(loaded, 16)
                            v.tensor_copy(edst[:, :], back[:, :, 1])
                            v.tensor_copy(pseudo[:, :, :], back[:, :, 2:2 + D])
                            ch.link(v.tensor_copy(ti[:, :], back[:, :, 0]))
                            ch.link(v.tensor_scalar(ti[:, :], ti[:, :], P - 1, None, ALU.bitwise_and))
                            ch.link(v.tensor_copy(srclo[:, :], ti[:, :]))
                            ch.link(v.tensor_scalar(dsthi[:, :], back[:, :, 0], 0.0, 1024.0, ALU.min, ALU.mult))
                            ch.link(v.tensor_tensor(srclo[:, :], srclo[:, :], dsthi[:, :], ALU.add))
                            ch.link(v.tensor_copy(ti[:, :], back[:, :, 1]))
                            ch.link(v.tensor_scalar(t2[:, :], ti[:, :], 7, None, ALU.arith_shift_right))
                            ch.link(v.tensor_scalar(ti[:, :], ti[:, :], P - 1, None, ALU.bitwise_and))
                            v.tensor_copy(dstlo[:, :], ti[:, :])
                            ch.link(v.tensor_copy(dsthi[:, :], t2[:, :]))
                            for k in range(KS):
                                ch.link(v.tensor_scalar(hat[:, :, :, k], pseudo[:, :, :], float(KS - 1), -float(k), ALU.mult, ALU.add))
                            hf = hat[:, :, :, :].rearrange("p t d k -> p (t d k)")
                            ch.link(v.scalar_tensor_tensor(hf, hf, -1.0, hf, ALU.mult, ALU.min))
                            ch.link(v.tensor_scalar(hf, hf, 1.0, 0.0, ALU.add, ALU.max))

                yz = sb("yz", [P, 2, HALF, KS, KS])
                basis = sb("basis", [P, 2, HALF, K + 1])
                own = sb("own", [P, 2, HALF, P])
                dlo = sb("dlo", [P, 2, HALF, P], BF16)
                dhi = sb("dhi", [P, 2, HALF, NT], BF16)
                stage_dst, store_dst = scatter("by_dst", dposi, drec, DREC, drecs)
                sums_ps = ps("sums_ps", [P, NT * P])
                deg_ps = ps("deg_ps", [P, BANK])
                made, used, step, summed, turn, loaded = (sem(n) for n in ("made", "used", "step3", "summed", "turn3", "loaded3"))
                with nc.Block() as block:

                    @block.sync
                    def _(sp):
                        sp.dma_start(w1s[:, :], w1.rearrange("k i o -> k (i o)")).then_inc(loaded, 16)
                        sp.dma_start(w3s[:, :], w3).then_inc(loaded, 16)
                        sp.dma_start(w4s[:, :], w4).then_inc(loaded, 16)
                        for n, (b, width) in enumerate(((b1, H1), (b2, H1), (b3, H1), (b4, D))):
                            sp.dma_start(bias[:, n, 0:width], b.partition_broadcast(P)).then_inc(loaded, 16)
                        sp.wait_ge(loaded, 7 * 16)

                    @block.gpsimd
                    def _(pool):
                        store_dst(pool)

                    @block.vector
                    def _(v):
                        ch = Chain(v, step)
                        ch.link(v.memset(basis[:, :, :, K:K + 1], 1.0))
                        base = ch.k

                        def make(i, g):
                            n = 2 * i + g
                            ch.off, ch.k = base + n, 0
                            v.wait_ge(used, n + 1)
                            s = bass.ds(n * HALF, HALF)
                            hx, hy, hz = (hat[:, s, d, :] for d in range(D))
                            ch.link(v.tensor_tensor(yz[:, g, :, :, :], bcast(hy, 3, KS), bcast(hz, 2, KS), ALU.mult))
                            yzf = yz[:, g, :, :, :].rearrange("p t y z -> p t (y z)")
                            v.tensor_tensor(basis[:, g, :, 0:K].rearrange("p t (x r) -> p t x r", x=KS),
                                            bcast(hx, 3, KS * KS), bcast(yzf, 2, KS), ALU.mult)
                            v.tensor_tensor(dhi[:, g, :, :], bcast(iota128[:, 0:NT], 1, HALF), bcast(dsthi[:, s], 2, NT), ALU.is_equal)
                            v.tensor_tensor(dlo[:, g, :, :], bcast(iota128[:, :], 1, HALF), bcast(dstlo[:, s], 2, P), ALU.is_equal)
                            v.tensor_tensor(own[:, g, :, :], bcast(iota128[:, :], 1, HALF), bcast(srclo[:, s], 2, P), ALU.is_equal).then_inc(made, 1)

                        with v.Fori(0, TRIPS) as i:
                            make(i, 0)
                            make(i, 1)
                        ch.off, ch.k = base + 2 * TRIPS, 0
                        v.wait_ge(summed, 1)
                        ch.link(v.tensor_copy(sums[:, :, :], sums_ps[:, :].rearrange("p (t k) -> p t k", t=NT)[:, :, 0:K + 1]))
                        v.tensor_scalar(rdeg[:, :], sums[:, :, K], 1.0, None, ALU.max)
                        ch.link(v.tensor_scalar(deg[:, :], deg_ps[:, 0:NT], 1.0, None, ALU.max))
                        v.tensor_scalar(has[:, :], deg_ps[:, 0:NT], 0.0, None, ALU.is_gt)
                        ch.link(v.reciprocal(rdeg[:, :], rdeg[:, :]))
                        v.reciprocal(rec_deg[:, :], deg[:, :]).then_inc(turn, 1)
                        v.wait_ge(turn, 2)
                        refine(v, ch, dis[:, :], deg[:, :], nt_tmp[:, :])
                        v.tensor_tensor(dis[:, :], dis[:, :], has[:, :], ALU.mult)

                    @block.scalar
                    def _(act):
                        stage_dst(act)
                        act.wait_ge(turn, 1)
                        act.activation(dis[:, :], rec_deg[:, :], ACT.Sqrt).then_inc(turn, 1)

                    @block.tensor
                    def _(pe):
                        pe.matmul(deg_ps[:, 0:NT], zeros[:, 0:P], zeros[:, 0:NT], start=True, stop=False)
                        clear(pe, sums_ps, NT * P)
                        pe.sem_inc(used, 2)

                        def add(n, g):
                            pe.wait_ge(made, n + 1)
                            for j in range(HALF):
                                pe.matmul(deg_ps[:, 0:NT], dlo[:, g, j, :], dhi[:, g, j, :], start=False, stop=False)
                                b = pe.value_load(bucket[0:1, bass.ds(n * HALF + j, 1)], min_val=0, max_val=NT - 1)
                                last = pe.matmul(sums_ps[:, bass.ds(b * P, K + 1)], own[:, g, j, :], basis[:, g, j, :],
                                                 start=False, stop=False, skip_group_check=True)
                            last.then_inc(used, 1)

                        with pe.Fori(0, TRIPS) as i:
                            add(2 * i, 0)
                            add(2 * i + 1, 1)
                        pe.matmul(deg_ps[:, 0:NT], zeros[:, 0:P], zeros[:, 0:NT], start=False, stop=True)
                        close(pe, sums_ps, NT * P).then_inc(summed, 1)

            linear("l1", lambda t: sums[:, t, 0:K], K, w1s[:, :], H1, h, scale=rdeg)
            bias_elu("e1", h[:, :, :], bias[:, 0, :])
            build_corners("z2", H1, h, w2, corners2)
            spline("s2", H1, corners2, h[:, :, :])
            bias_elu("e2", h[:, :, :], bias[:, 1, :])
            linear("l3", lambda t: h[:, t, :], H1, w3s[:, :], H1, h)
            bias_elu("e3", h[:, :, :], bias[:, 2, :])
            linear("l4", lambda t: h[:, t, :], H1, w4s[:, :], D, tn[:, 0, :, :])

            QUAD = 4
            own = sb("own4", [P, 2, 2, QUAD, P])
            pick = sb("pick", [P, 2, 2, QUAD * P])
            which = sb("which", [P, 2, 2, QUAD, NT])
            masked = sb("masked", [P, 2, QUAD, D, 2, NT])
            diff = sb("diff", [P, T, D])
            pick_ps = ps("pick_ps", [P, 2, 2, QUAD * P])
            all_ps = ps("all_ps", [P, 2, 2, BANK])
            made, turned, copied, picked, step, masks = (sem(n) for n in ("made4", "turned4", "copied4", "picked4", "step4", "masks4"))
            taken, totaled = sem("taken4"), sem("totaled4")
            trips = T // (2 * QUAD)
            with nc.Block() as block:

                @block.vector
                def _(v):
                    ch = Chain(v, step)
                    ch.link(v.tensor_tensor(tn[:, 0, :, :], tn[:, 0, :, :], bcast(bias[:, 3, 0:D], 1, NT), ALU.add))
                    ch.link(v.tensor_scalar(tn[:, 1, :, :], tn[:, 0, :, :], -1.0, None, ALU.mult))

                    def make(n, g):
                        v.wait_ge(turned, n + 1)
                        s = bass.ds(n * QUAD, QUAD)
                        it = bcast(iota128[:, :], 1, QUAD)
                        v.tensor_tensor(own[:, g, 0, :, :], it, bcast(dstlo[:, s], 2, P), ALU.is_equal)
                        v.tensor_tensor(own[:, g, 1, :, :], it, bcast(srclo[:, s], 2, P), ALU.is_equal).then_inc(made, 1)
                        v.wait_ge(taken, n + 1)
                        it = bcast(iota128[:, 0:NT], 1, QUAD)
                        v.tensor_tensor(which[:, g, 0, :, :], it, bcast(dsthi[:, s], 2, NT), ALU.is_equal)
                        v.tensor_tensor(which[:, g, 1, :, :], it, bcast(bucket[:, s], 2, NT), ALU.is_equal).then_inc(masks, 1)

                    def take(n, g):
                        v.wait_ge(picked, n + 3)
                        v.wait_ge(masks, n + 1)
                        v.wait_ge(totaled, n + 1)
                        for side in range(2):
                            a = all_ps[:, g, side, 0:QUAD * NT * D].rearrange("p (j b c) -> p j b c", j=QUAD, b=NT)
                            m = masked[:, g, :, :, side, :].rearrange("p j c b -> p j b c")
                            last = v.tensor_tensor(m, a, bcast(which[:, g, side, :, :], 3, D), ALU.mult)
                        last.then_inc(taken, 1)

                    def total(n, g):
                        v.wait_ge(taken, n + 3)
                        v.tensor_reduce(diff[:, bass.ds(n * QUAD, QUAD), :].rearrange("p t c -> p (t c)"),
                                        masked[:, g, :, :, :, :].rearrange("p j c s b -> p (j c) (s b)"), AX, ALU.add).then_inc(totaled, 1)

                    make(0, 0)
                    make(1, 1)
                    take(0, 0)
                    with v.Fori(0, trips - 1) as i:
                        make(2 * i + 2, 0)
                        total(2 * i, 0)
                        take(2 * i + 1, 1)
                        make(2 * i + 3, 1)
                        total(2 * i + 1, 1)
                        take(2 * i + 2, 0)
                    total(2 * trips - 2, 0)
                    take(2 * trips - 1, 1)
                    v.wait_ge(taken, 2 + 2 * trips)
                    ch.link(v.tensor_reduce(diff[:, T - QUAD:T, :].rearrange("p t c -> p (t c)"),
                                            masked[:, 1, :, :, :, :].rearrange("p j c s b -> p (j c) (s b)"), AX, ALU.add))
                    ch.link(v.tensor_tensor(pseudo[:, :, :], pseudo[:, :, :], diff[:, :, :], ALU.add))
                    v.tensor_scalar(pseudo[:, :, :], pseudo[:, :, :], 0.0, 1.0, ALU.max, ALU.min)

                @block.tensor
                def _(pe):
                    pe.sem_inc(turned, 2)

                    def turn(n, g):
                        pe.wait_ge(copied, n + 1)
                        pe.wait_ge(made, n + 1)
                        for side in range(2):
                            for j in range(QUAD):
                                last = pe.transpose(pick_ps[:, g, side, j * P:(j + 1) * P], own[:, g, side, j, :], ident[:, :])
                        last.then_inc(turned, 1)

                    def select(n, g):
                        pe.wait_ge(copied, n + 3)
                        pe.wait_ge(taken, n + 1)
                        for side in range(2):
                            tt = tn[:, side, :, :].rearrange("p t c -> p (t c)")
                            for j in range(QUAD):
                                last = pe.matmul(all_ps[:, g, side, j * NT * D:(j + 1) * NT * D], pick[:, g, side, j * P:(j + 1) * P], tt, start=True, stop=True)
                        last.then_inc(picked, 1)

                    turn(0, 0)
                    with pe.Fori(0, trips - 1) as i:
                        turn(2 * i + 1, 1)
                        select(2 * i, 0)
                        turn(2 * i + 2, 0)
                        select(2 * i + 1, 1)
                    turn(2 * trips - 1, 1)
                    select(2 * trips - 2, 0)
                    select(2 * trips - 1, 1)

                @block.scalar
                def _(act):
                    act.sem_inc(copied, 2)
                    act.sem_inc(taken, 2)
                    act.sem_inc(totaled, 2)
                    act.sem_inc(picked, 2)

                    def copy(n, g):
                        act.wait_ge(picked, n + 1)
                        act.wait_ge(turned, n + 3)
                        act.activation(pick[:, g, :, :], pick_ps[:, g, :, :], ACT.Copy).then_inc(copied, 1)

                    with act.Fori(0, trips) as i:
                        copy(2 * i, 0)
                        copy(2 * i + 1, 1)

        def norm_relu(name, u, result):
            with Phase():
                mean = sb(name + "_mean", [P, NT])
                var = sb(name + "_var", [P, NT])
                inv = sb(name + "_inv", [P, NT])
                tmp = sb(name + "_tmp", [P, NT])
                sq = sb(name + "_sq", [P, NT, C])
                step, turn = sem(name + "_step"), sem(name + "_turn")
                with nc.Block() as block:

                    @block.vector
                    def _(v):
                        ch = Chain(v, step)
                        ch.link(v.tensor_reduce(mean[:, :], u, AX, ALU.add))
                        ch.link(v.tensor_scalar(mean[:, :], mean[:, :], 1.0 / C, None, ALU.mult))
                        ch.link(v.tensor_tensor(result, u, bcast(mean[:, :], 2, C), ALU.subtract))
                        ch.link(v.tensor_tensor(sq[:, :, :], result, result, ALU.mult))
                        ch.link(v.tensor_reduce(var[:, :], sq[:, :, :], AX, ALU.add))
                        ch.link(v.tensor_scalar(var[:, :], var[:, :], 1.0 / C, EPS, ALU.mult, ALU.add))
                        v.reciprocal(tmp[:, :], var[:, :]).then_inc(turn, 1)
                        v.wait_ge(turn, 2)
                        refine(v, ch, inv[:, :], var[:, :], tmp[:, :])
                        ch.link(v.tensor_tensor(result, result, bcast(inv[:, :], 2, C), ALU.mult))
                        v.tensor_scalar(result, result, 0.0, None, ALU.max)

                    @block.scalar
                    def _(act):
                        act.wait_ge(turn, 1)
                        act.activation(inv[:, :], tmp[:, :], ACT.Sqrt).then_inc(turn, 1)

        with Phase():
            loaded, step = sem("loaded5"), sem("step5")
            with nc.Block() as block:

                @block.vector
                def _(v):
                    v.memset(xn[:, :, :], 0.0).then_inc(step, 1)

                @block.sync
                def _(sp):
                    sp.wait_ge(step, 1)
                    sp.dma_start(xn[:, 0:NT - 1, :], x[0:(NT - 1) * P, :].rearrange("(t p) c -> p t c", p=P)).then_inc(loaded, 16)
                    sp.dma_start(xn[0:NREST, NT - 1, :], x[(NT - 1) * P:N, :]).then_inc(loaded, 16)
                    sp.wait_ge(loaded, 32)

        with Phase():
            cur = sb("cur", [P, NT, C])
            total = sb("total", [P, NT, C])
            stage = sb("stage5", [P, 2, HALF], I32)
            gath = sb("gath", [P, 2, HALF, C])
            own = sb("own5", [P, 2, HALF, P])
            norm_relu("n0", xn[:, :, :], cur[:, :, :])
            with Phase():
                loaded, step = sem("loaded6"), sem("step6")
                with nc.Block() as block:

                    @block.sync
                    def _(sp):
                        sp.dma_start(dback[:, :, :].rearrange("p t r -> p (t r)"), drecs.rearrange("(p t) r -> p (t r)", p=P)).then_inc(loaded, 16)

                    @block.vector
                    def _(v):
                        ch = Chain(v, step)
                        v.tensor_copy(total[:, :, :], cur[:, :, :])
                        v.wait_ge(loaded, 16)
                        v.tensor_scalar(gsrc[:, :], dback[:, :, 0], 0.0, None, ALU.max)
                        ch.link(v.tensor_copy(dlow[:, :], dback[:, :, 1]))
                        ch.link(v.tensor_scalar(dlow[:, :], dlow[:, :], P - 1, None, ALU.bitwise_and))
                        ch.link(v.tensor_copy(dback[:, :, 0], dlow[:, :]))
                        ch.link(v.tensor_scalar(dback[:, :, 1], dback[:, :, 1], 0.0, 1024.0, ALU.min, ALU.mult))
                        ch.link(v.tensor_tensor(dback[:, :, 0], dback[:, :, 0], dback[:, :, 1], ALU.add))

            def propagate(layer):
                name = f"p{layer}"
                with Phase():
                    sums_ps = ps(name + "_sums_ps", [P, NT * C])
                    scaled, kept, summed, step = (sem(name + n) for n in ("_scaled", "_kept", "_summed", "_step"))
                    staged, made, used, gate, gate_a = (sem(name + n) for n in ("_staged", "_made", "_used", "_gate", "_gate_a"))
                    fetched = [sem(f"{name}_fetched{g}") for g in range(2)]
                    with nc.Block() as block:

                        @block.sync
                        def _(sp):
                            sp.wait_ge(scaled, 1)
                            sp.dma_start(ytab.rearrange("(t p) c -> p t c", p=P), cur[:, :, :]).then_inc(kept, 16)

                        @block.gpsimd
                        def _(pool):
                            pool.wait_ge(kept, 16)
                            with pool.Fori(0, TRIPS) as i:
                                for g in range(2):
                                    pool.wait_ge(staged, 2 * i + g + 1)
                                    pool.sem_inc(gate, 1)
                                    for j in range(HALF):
                                        pool.indirect_dma_start(gath[:, g, j, :], None, ytab,
                                                                bass.IndirectOffsetOnAxis(ap=stage[:, g, j:j + 1], axis=0)).then_inc(fetched[g], 16)

                        @block.scalar
                        def _(act):
                            def put(n, g):
                                act.activation(stage[:, g, :], gsrc[:, bass.ds(n * HALF, HALF)], ACT.Copy).then_inc(staged, 1)

                            put(0, 0)
                            put(1, 1)
                            with act.Fori(0, TRIPS - 1) as i:
                                for g in range(2):
                                    act.wait_ge(fetched[g], (i + 1) * (HALF * 16))
                                    act.wait_ge(used, 2 * i + g + 3)
                                    act.sem_inc(gate_a, 1)
                                    put(2 * i + g + 2, g)

                        @block.vector
                        def _(v):
                            ch = Chain(v, step)
                            v.tensor_tensor(cur[:, :, :], cur[:, :, :], bcast(dis[:, :], 2, C), ALU.mult).then_inc(scaled, 1)
                            with v.Fori(0, TRIPS) as i:
                                for g in range(2):
                                    n = 2 * i + g
                                    v.wait_ge(used, n + 1)
                                    v.tensor_tensor(own[:, g, :, :], bcast(iota128[:, :], 1, HALF),
                                                    bcast(dback[:, bass.ds(n * HALF, HALF), 0], 2, P), ALU.is_equal).then_inc(made, 1)
                            v.wait_ge(kept, 16)
                            v.wait_ge(summed, 1)
                            ch.link(v.tensor_tensor(cur[:, :, :], sums_ps[:, :].rearrange("p (t c) -> p t c", t=NT), bcast(dis[:, :], 2, C), ALU.mult))
                            ch.link(v.tensor_tensor(total[:, :, :], total[:, :, :], cur[:, :, :], ALU.add))
                            if layer == LAYERS - 1:
                                ch.link(v.tensor_scalar(total[:, :, :], total[:, :, :], 1.0 / (LAYERS + 1), None, ALU.mult))
                                v.tensor_tensor(xn[:, :, :], xn[:, :, :], total[:, :, :], ALU.add)

                        @block.tensor
                        def _(pe):
                            clear(pe, sums_ps, NT * C)
                            pe.sem_inc(used, 2)
                            with pe.Fori(0, TRIPS) as i:
                                for g in range(2):
                                    n = 2 * i + g
                                    pe.wait_ge(fetched[g], (i + 1) * (HALF * 16))
                                    pe.wait_ge(made, n + 1)
                                    for j in range(HALF):
                                        b = pe.value_load(dbucket[0:1, bass.ds(n * HALF + j, 1)], min_val=0, max_val=NT - 1)
                                        last = pe.matmul(sums_ps[:, bass.ds(b * C, C)], own[:, g, j, :], gath[:, g, j, :],
                                                         start=False, stop=False, skip_group_check=True)
                                    last.then_inc(used, 1)
                            close(pe, sums_ps, NT * C).then_inc(summed, 1)

            for layer in range(LAYERS):
                propagate(layer)

        norm_relu("n1", xn[:, :, :], h[:, :, 0:C])
        build_corners("z3", C, h, wc, corners3)
        spline("s3", C, corners3, h[:, :, 0:C])
        with Phase():
            bias3 = sb("bias3", [P, C])
            loaded, step, ready = sem("loaded7"), sem("step7"), sem("ready7")
            with nc.Block() as block:

                @block.vector
                def _(v):
                    ch = Chain(v, step)
                    r = h[:, :, 0:C]
                    v.wait_ge(loaded, 16)
                    ch.link(v.tensor_tensor(r, r, bcast(bias3[:, :], 1, NT), ALU.add))
                    v.tensor_tensor(xn[:, :, :], xn[:, :, :], r, ALU.add).then_inc(ready, 1)

                @block.sync
                def _(sp):
                    sp.dma_start(bias3[:, :], bc.partition_broadcast(P)).then_inc(loaded, 16)
                    sp.wait_ge(ready, 1)
                    sp.dma_start(out[0:(NT - 1) * P, :].rearrange("(t p) c -> p t c", p=P), xn[:, 0:NT - 1, :]).then_inc(loaded, 16)
                    sp.dma_start(out[(NT - 1) * P:N, :], xn[0:NREST, NT - 1, :]).then_inc(loaded, 16)
                    sp.wait_ge(loaded, 48)


_INS = ['x', 'src', 'dst', 'edge_attr_3', 'L1_gnn_stn1_w', 'L1_gnn_stn1_b', 'L1_gnn_stn2_w', 'L1_gnn_stn2_b',
        'L1_gnn_stn3_w', 'L1_gnn_stn3_b', 'L1_gnn_stn4_w', 'L1_gnn_stn4_b', 'L1_gnn_conv_w', 'L1_gnn_conv_b']
_OUTS = [((N, C), 'float32')]


def kernel(**inputs):
    import numpy as _np
    import concourse.bacc as _bacc
    from concourse import mybir as _mybir
    from concourse.bass_utils import run_bass_kernel_spmd as _run

    nc = _bacc.Bacc("TRN2", target_bir_lowering=False, num_devices=1)
    arrays, args = {}, []
    for name in _INS:
        a = _np.ascontiguousarray(inputs[name])
        arrays[f"in_{name}_dram"] = a
        args.append(nc.dram_tensor(f"in_{name}_dram", a.shape, _mybir.dt.from_np(a.dtype), kind="ExternalInput").ap())
    for i, (shape, dtype) in enumerate(_OUTS):
        dt = _mybir.dt.from_np(_np.dtype(dtype))
        args.append(nc.dram_tensor(f"out_{i}_dram", shape, dt, kind="ExternalOutput").ap())
    gnn(nc, *args)
    r = _run(nc, [arrays], core_ids=[0])
    got = tuple(r.results[0][f"out_{i}_dram"] for i in range(len(_OUTS)))
    return got[0]
```

```python
from contextlib import ExitStack

import concourse.bass as bass
from concourse import mybir

F32 = mybir.dt.float32
BF16 = mybir.dt.bfloat16
I32 = mybir.dt.int32
I16 = mybir.dt.int16
ALU = mybir.AluOpType
ACT = mybir.ActivationFunctionType
AX = mybir.AxisListType.X

P = 128
N = 3125
NT = -(-N // P)
NP = NT * P
NREST = N - (NT - 1) * P
E = 100000
EP = 125
EC = E // EP
HALF = 8
BODY = 2 * HALF
T = -(-(E // P + NT) // BODY) * BODY
TRIPS = T // BODY
HALVES = T // HALF
D = 3
KS = 5
K = KS ** D
C = 32
H1 = 64
LAYERS = 3
REC = 8
DREC = 2
CELLS = 4 * 4 * KS
BANK = 512
EPS = 1e-5


class Chain:

    def __init__(self, eng, sem):
        self.eng, self.sem, self.base, self.off, self.k = eng, sem, 0, 0, 0

    def link(self, ins):
        ins.then_inc(self.sem, 1)
        self.k += 1
        self.eng.wait_ge(self.sem, self.off + self.k)


def bcast(ap, dim, n):
    v = ap.unsqueeze(dim)
    shape = list(v.shape)
    shape[dim] = n
    return v.broadcast_to(shape)


def gnn(nc, x, src, dst, edge_attr_3, w1, b1, w2, b2, w3, b3, w4, b4, wc, bc, out):
    recs = nc.dram_tensor("recs", (P * T, REC), F32, kind="Internal").ap()
    corners2 = nc.dram_tensor("corners2", (NP * CELLS, 4 * H1), F32, kind="Internal").ap()
    corners3 = nc.dram_tensor("corners3", (NP * CELLS, 4 * C), F32, kind="Internal").ap()
    drecs = nc.dram_tensor("drecs", (P * T, DREC), F32, kind="Internal").ap()
    ytab = nc.dram_tensor("ytab", (NP, C), F32, kind="Internal").ap()

    with ExitStack() as whole:
        scopes = [whole]

        def sb(name, shape, dt=F32):
            return scopes[-1].enter_context(nc.sbuf_tensor(name, shape, dt))

        def ps(name, shape, dt=F32):
            return scopes[-1].enter_context(nc.psum_tensor(name, shape, dt))

        def sem(name):
            return scopes[-1].enter_context(nc.semaphore(name))

        class Phase:

            def __enter__(self):
                scopes.append(ExitStack())
                scopes[-1].__enter__()

            def __exit__(self, *a):
                scopes.pop().__exit__(*a)

        iota128 = sb("iota128", [P, P])
        pidx = sb("pidx", [P, 1])
        ident = sb("ident", [P, P])
        ones = sb("ones", [P, P])
        zeros = sb("zeros", [P, BANK], BF16)
        bucket = sb("bucket", [P, T], I32)
        srclo = sb("srclo", [P, T])
        edst = sb("edst", [P, T])
        dstlo = sb("dstlo", [P, T])
        dsthi = sb("dsthi", [P, T])
        pseudo = sb("pseudo", [P, T, D])
        dbucket = sb("dbucket", [P, T], I32)
        dback = sb("dback", [P, T, DREC])
        gsrc = sb("gsrc", [P, T], I32)
        dposi = sb("dposi", [EP, EC], I32)
        drec = sb("drec", [EP, EC, DREC])
        rdeg = sb("rdeg", [P, NT])
        dis = sb("dis", [P, NT])
        xn = sb("xn", [P, NT, C])
        h = sb("h", [P, NT, H1])
        cur = sb("cur", [P, NT, C])
        total = sb("total", [P, NT, C])

        def scatter(name, posi, rec, width, recs):
            stage_i = sb(name + "_stage_i", [EP, BODY], I32)
            stage_r = sb(name + "_stage_r", [EP, BODY, width])
            staged, gate, gate_p = sem(name + "_staged"), sem(name + "_gate"), sem(name + "_gate_p")
            stored = [sem(f"{name}_stored{g}") for g in range(2)]
            turns = EC // BODY

            def stage(act):
                def put(turn, g):
                    act.activation(stage_i[:, g * HALF:(g + 1) * HALF], posi[:, bass.ds(turn * BODY + g * HALF, HALF)], ACT.Copy)
                    act.activation(stage_r[:, g * HALF:(g + 1) * HALF, :], rec[:, bass.ds(turn * BODY + g * HALF, HALF), :], ACT.Copy).then_inc(staged, 1)

                put(0, 0)
                put(0, 1)
                with act.Fori(0, turns - 1) as i:
                    for g in range(2):
                        act.wait_ge(stored[g], (i + 1) * (16 * HALF))
                        act.sem_inc(gate, 1)
                        put(i + 1, g)

            def store(pool):
                with pool.Fori(0, turns) as i:
                    for g in range(2):
                        pool.wait_ge(staged, 2 * i + g + 1)
                        pool.sem_inc(gate_p, 1)
                        for j in range(g * HALF, (g + 1) * HALF):
                            pool.indirect_dma_start(recs, bass.IndirectOffsetOnAxis(ap=stage_i[:, j:j + 1], axis=0),
                                                    stage_r[:, j, :], None).then_inc(stored[g], 16)
                for g in range(2):
                    pool.wait_ge(stored[g], turns * HALF * 16)

            return stage, store

        with Phase():
            esi = sb("esi", [EP, EC], I32)
            edi = sb("edi", [EP, EC], I32)
            eps_in = sb("eps_in", [EP, EC, D])
            hi_i = sb("hi_i", [EP, EC], I32)
            key = sb("key", [EP, EC])
            eq = sb("eq", [EP, 2, EC])
            cum = sb("cum", [EP, 2, EC])
            zero = sb("zero", [EP, EC])
            mine = sb("mine", [EP, 2, EC])
            pos = sb("pos", [EP, EC])
            posi = sb("posi", [EP, EC], I32)
            low_i = sb("low_i", [EP, EC], I32)
            high_i = sb("high_i", [EP, EC], I32)
            posf = sb("posf", [EP, EC])
            rec = sb("rec", [EP, EC, REC])
            pad = sb("pad", [P, T, REC])
            dpad = sb("dpad", [P, T, DREC])
            tot = sb("tot", [EP, 2, NT])
            tri = sb("tri", [P, P])
            cnti = sb("cnti", [P, NT], I32)
            tiles = sb("tiles", [P, NT])
            tend = sb("tend", [P, NT])
            tstart = sb("tstart", [P, NT])
            off = sb("off", [EP, NT])
            iotat = sb("iotat", [P, T])
            bf = sb("bf", [P, 2, T])
            count_ps = ps("count_ps", [P, 2, 2, BANK])
            loaded, iotas, step, tot_ready, counts = (sem(n) for n in ("loaded", "iotas", "step", "tot_ready", "counts"))
            padded, pad_ready, ranked = (sem(n) for n in ("padded", "pad_ready", "ranked"))
            stage_src, store_src = scatter("by_src", posi, rec, REC, recs)
            with nc.Block() as block:

                @block.sync
                def _(sp):
                    sp.dma_start(esi[:, :], src.rearrange("(p c) -> p c", p=EP)).then_inc(loaded, 16)
                    sp.dma_start(edi[:, :], dst.rearrange("(p c) -> p c", p=EP)).then_inc(loaded, 16)
                    sp.dma_start(eps_in[:, :, :], edge_attr_3.rearrange("(p c) d -> p c d", p=EP)).then_inc(loaded, 16)
                    sp.wait_ge(pad_ready, 1)
                    sp.dma_start(recs.rearrange("(p t) r -> p (t r)", p=P), pad[:, :, :].rearrange("p t r -> p (t r)")).then_inc(padded, 16)
                    sp.dma_start(drecs.rearrange("(p t) r -> p (t r)", p=P), dpad[:, :, :].rearrange("p t r -> p (t r)")).then_inc(padded, 16)

                @block.tensor
                def _(pe):
                    for k in range(2):
                        pe.wait_ge(tot_ready, k + 1)
                        nc.tensor.matmul(count_ps[0:EP, k, 0, 0:NT], tri[0:EP, 0:EP], tot[:, k, :], start=True, stop=True)
                        nc.tensor.matmul(count_ps[:, k, 1, 0:NT], ones[0:EP, :], tot[:, k, :], start=True, stop=True).then_inc(counts, 1)

                @block.scalar
                def _(act):
                    act.wait_ge(ranked, 1)
                    stage_src(act)

                @block.gpsimd
                def _(pool):
                    pool.iota(iota128[:, :], [[1, P]], base=0, channel_multiplier=0, allow_small_or_imprecise_dtypes=True).then_inc(iotas, 1)
                    pool.iota(pidx[:, :], [[0, 1]], base=0, channel_multiplier=1, allow_small_or_imprecise_dtypes=True).then_inc(iotas, 1)
                    pool.iota(iotat[:, :], [[1, T]], base=0, channel_multiplier=0, allow_small_or_imprecise_dtypes=True).then_inc(iotas, 1)
                    pool.wait_ge(padded, 32)
                    store_src(pool)

                @block.vector
                def _(v):
                    ch = Chain(v, step)

                    def rank(k, node, row, bucket_of):
                        ch.link(v.tensor_scalar(hi_i[:, :], node[:, :], 7, None, ALU.arith_shift_right))
                        ch.link(v.tensor_copy(key[:, :], hi_i[:, :]))
                        for b in range(NT):
                            last = v.tensor_scalar(eq[:, b % 2, :], key[:, :], float(b), None, ALU.is_equal, ALU.add, accum_out=tot[:, k, b:b + 1])
                            ch.link(last)
                        v.memset(pos[:, :], 0.0)
                        v.memset(bf[:, 1, :], -1.0).then_inc(tot_ready, 1)
                        v.wait_ge(counts, k + 1)
                        ch.link(v.tensor_scalar(cnti[:, :], count_ps[:, k, 1, 0:NT], float(P - 1), None, ALU.add))
                        ch.link(v.tensor_scalar(cnti[:, :], cnti[:, :], 7, None, ALU.arith_shift_right))
                        ch.link(v.tensor_copy(tiles[:, :], cnti[:, :]))
                        ch.link(v.tensor_tensor_scan(tend[:, :], ones[:, 0:NT], tiles[:, :], 0.0, ALU.mult, ALU.add))
                        ch.link(v.tensor_tensor(tstart[:, :], tend[:, :], tiles[:, :], ALU.subtract))
                        ch.link(v.tensor_scalar(off[:, :], tstart[0:EP, :], float(P), -1.0, ALU.mult, ALU.add))
                        ch.link(v.tensor_tensor(off[:, :], count_ps[0:EP, k, 0, 0:NT], off[:, :], ALU.add))
                        for b in range(NT):
                            q = b % 2
                            ch.link(v.tensor_scalar(eq[:, q, :], key[:, :], float(b), None, ALU.is_equal))
                            ch.link(v.tensor_tensor_scan(cum[:, q, :], eq[:, q, :], zero[:, :], 0.0, ALU.add, ALU.add))
                            ch.link(v.scalar_tensor_tensor(mine[:, q, :], cum[:, q, :], off[:, b:b + 1], eq[:, q, :], ALU.add, ALU.mult))
                            ch.link(v.tensor_tensor(pos[:, :], pos[:, :], mine[:, q, :], ALU.add))
                        ch.link(v.tensor_copy(low_i[:, :], pos[:, :]))
                        ch.link(v.tensor_scalar(high_i[:, :], low_i[:, :], 7, None, ALU.arith_shift_right))
                        ch.link(v.tensor_scalar(low_i[:, :], low_i[:, :], P - 1, None, ALU.bitwise_and))
                        v.tensor_copy(posf[:, :], low_i[:, :])
                        ch.link(v.tensor_copy(mine[:, 0, :], high_i[:, :]))
                        ch.link(v.scalar_tensor_tensor(pos[:, :], posf[:, :], float(T), mine[:, 0, :], ALU.mult, ALU.add))
                        v.tensor_copy(row[:, :], pos[:, :]).then_inc(ranked, 1)
                        for b in range(NT):
                            ch.link(v.scalar_tensor_tensor(bf[:, b % 2, :], iotat[:, :], tstart[:, b:b + 1], bf[:, (b + 1) % 2, :], ALU.is_ge, ALU.add))
                        ch.link(v.tensor_copy(bucket_of[:, :], bf[:, (NT - 1) % 2, :]))

                    ch.link(v.memset(pad[:, :, :], 0.0))
                    v.memset(dpad[:, :, :], -1.0)
                    v.memset(pad[:, :, 0:2], -1.0).then_inc(pad_ready, 1)
                    v.memset(ones[:, :], 1.0)
                    v.memset(zero[:, :], 0.0)
                    v.memset(zeros[:, :], 0.0)
                    ch.link(v.memset(rec[:, :, :], 0.0))
                    v.wait_ge(iotas, 3)
                    v.tensor_scalar(ident[:, :], iota128[:, :], pidx[:, 0:1], None, ALU.is_equal)
                    v.tensor_scalar(tri[:, :], iota128[:, :], pidx[:, 0:1], None, ALU.is_gt)
                    v.wait_ge(loaded, 48)
                    for k, e in enumerate((esi, edi)):
                        v.tensor_copy(rec[:, :, k], e[:, :])
                        v.tensor_copy(drec[:, :, k], e[:, :])
                    v.tensor_copy(rec[:, :, 2:2 + D], eps_in[:, :, :])
                    rank(0, esi, posi, bucket)
                    rank(1, edi, dposi, dbucket)

        def corner_tables(v, ch, i0, fr, fr0, weight, cidx, tmp, s):
            ch.link(v.tensor_scalar(fr[:, :, :], pseudo[:, s, :], float(KS - 1), None, ALU.mult))
            ch.link(v.tensor_scalar(i0[:, :, :], fr[:, :, :], 1.0, None, ALU.is_ge))
            for knot in range(2, KS - 1):
                ch.link(v.scalar_tensor_tensor(i0[:, :, :], fr[:, :, :], float(knot), i0[:, :, :], ALU.is_ge, ALU.add))
            ch.link(v.tensor_tensor(fr[:, :, :], fr[:, :, :], i0[:, :, :], ALU.subtract))
            ch.link(v.tensor_scalar(fr0[:, :, :], fr[:, :, :], -1.0, 1.0, ALU.mult, ALU.add))
            w = weight[:, s, :].rearrange("p t (y x z) -> p t y x z", y=2, x=2)
            ends = (fr0, fr)
            for cy in range(2):
                for cx in range(2):
                    v.tensor_tensor(w[:, :, cy, cx, 1], ends[cx][:, :, 0], ends[cy][:, :, 1], ALU.mult)
            for cy in range(2):
                for cx in range(2):
                    last = v.tensor_tensor(w[:, :, cy, cx, 0], ends[cx][:, :, 0], ends[cy][:, :, 1], ALU.mult)
            ch.link(last)
            for cz in range(2):
                for c in range(4):
                    cc = w[:, :, c // 2, c % 2, cz]
                    last = v.tensor_tensor(cc, cc, ends[cz][:, :, 2], ALU.mult)
            ch.link(last)
            ch.link(v.tensor_scalar(tmp[:, :], edst[:, s], 0.0, float(CELLS), ALU.max, ALU.mult))
            for d, stride in ((0, 4 * KS), (1, 1), (2, KS)):
                ch.link(v.scalar_tensor_tensor(tmp[:, :], i0[:, :, d], float(stride), tmp[:, :], ALU.mult, ALU.add))
            ch.link(v.tensor_copy(cidx[:, s], tmp[:, :]))

        def corner_buffers(name):
            return sb(name + "_weight", [P, T, 8]), sb(name + "_cidx", [P, T], I32)

        def refine(v, ch, s, a, tmp):
            ch.link(v.tensor_tensor(tmp, s, s, ALU.mult))
            ch.link(v.tensor_tensor(tmp, tmp, a, ALU.mult))
            ch.link(v.tensor_scalar(tmp, tmp, -0.5, 1.5, ALU.mult, ALU.add))
            ch.link(v.tensor_tensor(s, s, tmp, ALU.mult))

        def clear(pe, sums, columns):
            for c in range(0, columns, BANK):
                pe.matmul(sums[:, c:min(c + BANK, columns)], zeros[:, 0:P], zeros[:, 0:min(BANK, columns - c)], start=True, stop=False)

        def close(pe, sums, columns):
            for c in range(0, columns, BANK):
                last = pe.matmul(sums[:, c:min(c + BANK, columns)], zeros[:, 0:P], zeros[:, 0:min(BANK, columns - c)], start=False, stop=True)
            return last

        def linear(name, tile_of, kin, w, kout, result, scale=None):
            G = 5
            with Phase():
                turned = sb(name + "_turned", [kin, G * P])
                turned_ps = ps(name + "_turned_ps", [P, 2 * BANK])
                out_ps = ps(name + "_out_ps", [P, BANK])
                in_psum, in_sbuf, multiplied, kept = (sem(name + x) for x in ("_t", "_s", "_m", "_k"))
                with nc.Block() as block:

                    @block.tensor
                    def _(pe):
                        for i in range(NT // G):
                            for j in range(G):
                                last = pe.transpose(turned_ps[0:kin, j * P:(j + 1) * P], tile_of(i * G + j), ident[:, :])
                            last.then_inc(in_psum, 1)
                            pe.wait_ge(in_sbuf, i + 1)
                            pe.wait_ge(kept, i + 1)
                            for j in range(G):
                                last = pe.matmul(out_ps[:, j * kout:(j + 1) * kout], turned[:, j * P:(j + 1) * P], w, start=True, stop=True)
                            last.then_inc(multiplied, 1)

                    @block.scalar
                    def _(act):
                        with act.Fori(0, NT // G) as i:
                            act.wait_ge(in_psum, i + 1)
                            act.activation(turned[:, :], turned_ps[0:kin, 0:G * P], ACT.Copy).then_inc(in_sbuf, 1)

                    @block.vector
                    def _(v):
                        v.sem_inc(kept, 1)
                        with v.Fori(0, NT // G) as i:
                            v.wait_ge(multiplied, i + 1)
                            r = result[:, bass.ds(i * G, G), :]
                            o = out_ps[:, 0:G * kout].rearrange("p (t c) -> p t c", t=G)
                            if scale is None:
                                v.tensor_copy(r, o).then_inc(kept, 1)
                            else:
                                v.tensor_tensor(r, o, bcast(scale[:, bass.ds(i * G, G)], 2, kout), ALU.mult).then_inc(kept, 1)

        def bias_elu(name, u, bias):
            with Phase():
                low = sb(name + "_low", [P, NT, H1])
                step, cut, raised = sem(name + "_step"), sem(name + "_cut"), sem(name + "_raised")
                with nc.Block() as block:

                    @block.vector
                    def _(v):
                        ch = Chain(v, step)
                        ch.link(v.tensor_tensor(u, u, bcast(bias, 1, NT), ALU.add))
                        v.tensor_scalar(low[:, :, :], u, 0.0, None, ALU.min).then_inc(cut, 1)
                        v.wait_ge(raised, 1)
                        ch.link(v.tensor_scalar(u, u, 0.0, -1.0, ALU.max, ALU.add))
                        v.tensor_tensor(u, u, low[:, :, :], ALU.add)

                    @block.scalar
                    def _(act):
                        act.wait_ge(cut, 1)
                        act.activation(low[:, :, :], low[:, :, :], ACT.Exp).then_inc(raised, 1)

        def norm_relu(name, u, result):
            with Phase():
                mean = sb(name + "_mean", [P, NT])
                var = sb(name + "_var", [P, NT])
                inv = sb(name + "_inv", [P, NT])
                tmp = sb(name + "_tmp", [P, NT])
                sq = sb(name + "_sq", [P, NT, C])
                step, turn = sem(name + "_step"), sem(name + "_turn")
                with nc.Block() as block:

                    @block.vector
                    def _(v):
                        ch = Chain(v, step)
                        ch.link(v.tensor_reduce(mean[:, :], u, AX, ALU.add))
                        ch.link(v.tensor_scalar(mean[:, :], mean[:, :], 1.0 / C, None, ALU.mult))
                        ch.link(v.tensor_tensor(result, u, bcast(mean[:, :], 2, C), ALU.subtract))
                        ch.link(v.tensor_tensor(sq[:, :, :], result, result, ALU.mult))
                        ch.link(v.tensor_reduce(var[:, :], sq[:, :, :], AX, ALU.add))
                        ch.link(v.tensor_scalar(var[:, :], var[:, :], 1.0 / C, EPS, ALU.mult, ALU.add))
                        v.reciprocal(tmp[:, :], var[:, :]).then_inc(turn, 1)
                        v.wait_ge(turn, 2)
                        refine(v, ch, inv[:, :], var[:, :], tmp[:, :])
                        ch.link(v.tensor_tensor(result, result, bcast(inv[:, :], 2, C), ALU.mult))
                        v.tensor_scalar(result, result, 0.0, None, ALU.max)

                    @block.scalar
                    def _(act):
                        act.wait_ge(turn, 1)
                        act.activation(inv[:, :], tmp[:, :], ACT.Sqrt).then_inc(turn, 1)

        def buckets(table, n):
            return nc.values_load_multi_w_load_instructions(table[0:1, bass.ds(n * HALF, HALF)], engines=[mybir.EngineType.PE],
                                                            min_val=0, max_val=NT - 1)[1]

        class Layer:

            def __init__(self, layer):
                self.layer = layer
                name = f"p{layer}"
                self.stage = sb(name + "_stage", [P, 2, HALF], I32)
                self.gath = sb(name + "_gath", [P, 2, HALF, C])
                self.own = sb(name + "_own", [P, 2, HALF, P])
                self.sums_ps = ps(name + "_sums_ps", [P, 2 * BANK])
                self.scaled, self.kept, self.summed, self.step = (sem(name + n) for n in ("_scaled", "_kept", "_summed", "_step"))
                self.staged, self.made, self.used, self.gate, self.gate_a = (sem(name + n) for n in ("_staged", "_made", "_used", "_gate", "_gate_a"))
                self.fetched = [sem(f"{name}_fetched{g}") for g in range(2)]

            def sp_begin(self, sp):
                sp.wait_ge(self.scaled, 1)
                sp.dma_start(ytab.rearrange("(t p) c -> p t c", p=P), cur[:, :, :]).then_inc(self.kept, 16)

            def pool_begin(self, pool):
                pool.wait_ge(self.kept, 16)

            def pool(self, pool, n, trip, g):
                pool.wait_ge(self.staged, n + 1)
                pool.sem_inc(self.gate, 1)
                pool.wait_ge(self.used, n + 1)
                pool.sem_inc(self.gate, 1)
                for j in range(HALF):
                    pool.indirect_dma_start(self.gath[:, g, j, :], None, ytab,
                                            bass.IndirectOffsetOnAxis(ap=self.stage[:, g, j:j + 1], axis=0)).then_inc(self.fetched[g], 16)

            def put(self, act, n, g):
                act.activation(self.stage[:, g, :], gsrc[:, bass.ds(n * HALF, HALF)], ACT.Copy).then_inc(self.staged, 1)

            def act_begin(self, act):
                self.put(act, 0, 0)
                self.put(act, 1, 1)

            def act(self, act, n, trip, g):
                act.wait_ge(self.fetched[g], (trip + 1) * (HALF * 16))
                act.sem_inc(self.gate_a, 1)
                self.put(act, n + 2, g)

            def dve_begin(self, v):
                v.tensor_tensor(cur[:, :, :], cur[:, :, :], bcast(dis[:, :], 2, C), ALU.mult).then_inc(self.scaled, 1)

            def dve(self, v, n, trip, g):
                v.wait_ge(self.used, n + 1)
                v.tensor_tensor(self.own[:, g, :, :], bcast(iota128[:, :], 1, HALF),
                                bcast(dback[:, bass.ds(n * HALF, HALF), 0], 2, P), ALU.is_equal).then_inc(self.made, 1)

            def dve_end(self, v):
                ch = Chain(v, self.step)
                v.wait_ge(self.kept, 16)
                v.wait_ge(self.summed, 1)
                ch.link(v.tensor_tensor(cur[:, :, :], self.sums_ps[:, 0:NT * C].rearrange("p (t c) -> p t c", t=NT), bcast(dis[:, :], 2, C), ALU.mult))
                ch.link(v.tensor_tensor(total[:, :, :], total[:, :, :], cur[:, :, :], ALU.add))
                if self.layer == LAYERS - 1:
                    ch.link(v.tensor_scalar(total[:, :, :], total[:, :, :], 1.0 / (LAYERS + 1), None, ALU.mult))
                    v.tensor_tensor(xn[:, :, :], xn[:, :, :], total[:, :, :], ALU.add)

            def pe_begin(self, pe):
                clear(pe, self.sums_ps, NT * C)
                pe.sem_inc(self.used, 2)

            def pe(self, pe, n, trip, g):
                tiles = buckets(dbucket, n)
                pe.wait_ge(self.fetched[g], (trip + 1) * (HALF * 16))
                pe.wait_ge(self.made, n + 1)
                for j in range(HALF):
                    last = pe.matmul(self.sums_ps[:, bass.ds(tiles[j] * C, C)], self.own[:, g, j, :], self.gath[:, g, j, :],
                                     start=False, stop=False, skip_group_check=True)
                last.then_inc(self.used, 1)

            def pe_end(self, pe):
                close(pe, self.sums_ps, NT * C).then_inc(self.summed, 1)

        def propagate(n, weight, cidx):
            with Phase():
                alone = Layer(n)
                i0, fr, fr0 = (sb(f"tables_{x}", [P, BODY, D]) for x in ("i0", "fr", "fr0"))
                tmp = sb("tables_tmp", [P, BODY])
                step = sem("tables_step")
                with nc.Block() as block:

                    @block.sync
                    def _(sp):
                        alone.sp_begin(sp)

                    @block.gpsimd
                    def _(pool):
                        alone.pool_begin(pool)
                        with pool.Fori(0, TRIPS) as i:
                            for g in range(2):
                                alone.pool(pool, 2 * i + g, i, g)

                    @block.scalar
                    def _(act):
                        alone.act_begin(act)
                        with act.Fori(0, TRIPS - 1) as i:
                            for g in range(2):
                                alone.act(act, 2 * i + g, i, g)

                    @block.vector
                    def _(v):
                        ch = Chain(v, step)

                        def tables(trip):
                            corner_tables(v, ch, i0, fr, fr0, weight, cidx, tmp, bass.ds(trip * BODY, BODY))

                        alone.dve_begin(v)
                        tables(0)
                        per_trip = ch.k
                        with v.Fori(0, TRIPS - 1) as i:
                            for g in range(2):
                                alone.dve(v, 2 * i + g, i, g)
                            ch.off, ch.k = (i + 1) * per_trip, 0
                            tables(i + 1)
                        for g in range(2):
                            alone.dve(v, HALVES - 2 + g, TRIPS - 1, g)
                        alone.dve_end(v)

                    @block.tensor
                    def _(pe):
                        alone.pe_begin(pe)
                        with pe.Fori(0, TRIPS) as i:
                            for g in range(2):
                                alone.pe(pe, 2 * i + g, i, g)
                        alone.pe_end(pe)

        def build_corners(name, f, nodes, w_dram, table, layer=None):
            G = 5
            row = KS * f
            parts = ((0, 3), (3, 2))
            banks = -(-3 * row // BANK)
            with Phase():
                w = sb(name + "_w", [f, K * f])
                turned = sb(name + "_turned", [f, NT * P])
                with Phase():
                    turned_ps = ps(name + "_turned_ps", [P, 2, 2 * BANK])
                    in_psum, in_sbuf, loaded = (sem(name + x) for x in ("_t", "_s", "_l"))
                    with nc.Block() as block:

                        @block.sync
                        def _(sp):
                            sp.dma_start(w[:, :].rearrange("i (k o) -> i k o", k=K), w_dram.rearrange("k i o -> i k o")).then_inc(loaded, 16)
                            sp.wait_ge(loaded, 16)

                        @block.tensor
                        def _(pe):
                            for i in range(NT // G):
                                if i >= 2:
                                    pe.wait_ge(in_sbuf, i - 1)
                                for j in range(G):
                                    last = pe.transpose(turned_ps[0:f, i % 2, j * P:(j + 1) * P], nodes[:, i * G + j, 0:f], ident[:, :])
                                last.then_inc(in_psum, 1)

                        @block.scalar
                        def _(act):
                            for i in range(NT // G):
                                act.wait_ge(in_psum, i + 1)
                                act.activation(turned[:, i * G * P:(i + 1) * G * P], turned_ps[0:f, i % 2, 0:G * P], ACT.Copy).then_inc(in_sbuf, 1)

                mine = sb(name + "_mine", [f, P])
                cube = sb(name + "_cube", [P, 4, 4, KS, 2, 2 * f])
                plane_ps = ps(name + "_plane_ps", [P, 2, banks * BANK])
                planes, by_act, by_dve, placed, gate_a = (sem(name + x) for x in ("_planes", "_by_act", "_by_dve", "_placed", "_gate_a"))
                stored = [sem(f"{name}_stored{i}") for i in range(4)]
                rows = table.rearrange("(t p x r) c -> t p x (r c)", t=NT, p=P, x=4)
                beside = None if layer is None else Layer(layer)

                def spread(copy, part, x, cx):
                    y, n = parts[part]
                    knots = plane_ps[:, part, 0:n * row].rearrange("p (y z o) -> p y z o", y=n, z=KS)
                    for cz in range(2):
                        last = copy(cube[:, x, :, y:y + n, cx, cz * f:(cz + 1) * f], knots[:, :, cz:cz + 4, :].rearrange("p y z o -> p z y o"))
                    return last

                with nc.Block() as block:

                    if beside:
                        @block.gpsimd
                        def _(pool):
                            beside.pool_begin(pool)
                            with pool.Fori(0, TRIPS) as i:
                                for g in range(2):
                                    beside.pool(pool, 2 * i + g, i, g)

                    @block.tensor
                    def _(pe):
                        if beside:
                            beside.pe_begin(pe)
                        with pe.Fori(0, NT) as i:
                            pe.wait_ge(placed, i + 1)
                            for kx in range(KS):
                                for part, (y, n) in enumerate(parts):
                                    if kx == 0:
                                        pe.wait_ge(by_dve, 8 * i + (part + 1))
                                    else:
                                        pe.wait_ge(by_act, 8 * i + (2 * kx + part + 1))
                                    for c in range(0, n * row, BANK):
                                        m = min(BANK, n * row - c)
                                        at = (kx * KS + y) * row + c
                                        last = pe.matmul(plane_ps[:, part, c:c + m], mine[:, :], w[:, at:at + m], start=True, stop=True)
                                    last.then_inc(planes, 1)
                                if beside and kx < 4:
                                    beside.pe(pe, 4 * i + kx, 2 * i + kx // 2, kx % 2)
                        if beside:
                            for k in range(4 * NT, HALVES):
                                beside.pe(pe, k, k // 2, k % 2)
                            beside.pe_end(pe)

                    def near(act, i, first):
                        if not first:
                            act.wait_ge(planes, i * (2 * KS))
                            act.sem_inc(gate_a, 1)
                        act.activation(mine[:, :], turned[:, bass.ds(i * P, P)], ACT.Copy).then_inc(placed, 1)
                        for kx in range(4):
                            for part in range(2):
                                if not first and part == 0:
                                    act.wait_ge(stored[kx], i * 16)
                                    if kx:
                                        act.wait_ge(by_dve, 8 * i + (2 * kx - 6))
                                act.wait_ge(planes, 2 * KS * i + (2 * kx + part + 1))
                                act.sem_inc(gate_a, 1)
                                spread(lambda o, s: act.activation(o, s, ACT.Copy), part, kx, 0).then_inc(by_act, 1)
                            if beside:
                                beside.act(act, 4 * i + kx, 2 * i + kx // 2, kx % 2)

                    def far(v, i, first):
                        for kx in range(1, KS):
                            if beside:
                                beside.dve(v, 4 * i + kx, 2 * i + kx // 2, kx % 2)
                            if not first:
                                v.wait_ge(stored[kx - 1], i * 16)
                            if kx < 4:
                                v.wait_ge(by_act, 8 * i + (2 * kx + 4))
                                v.tensor_copy(cube[:, kx - 1, :, :, 1, :], cube[:, kx, :, :, 0, :]).then_inc(by_dve, 2)
                            else:
                                for part in range(2):
                                    v.wait_ge(planes, 2 * KS * i + (2 * kx + part + 1))
                                    spread(v.tensor_copy, part, kx - 1, 1).then_inc(by_dve, 1)

                    @block.scalar
                    def _(act):
                        act.sem_inc(by_act, 2)
                        if beside:
                            beside.act_begin(act)
                        near(act, 0, True)
                        with act.Fori(1, NT) as i:
                            near(act, i, False)

                    @block.vector
                    def _(v):
                        v.sem_inc(by_dve, 2)
                        if beside:
                            beside.dve_begin(v)
                            beside.dve(v, 0, 0, 0)
                        far(v, 0, True)
                        with v.Fori(1, NT) as i:
                            far(v, i, False)
                        if beside:
                            for k in range(4 * NT + 1, HALVES):
                                beside.dve(v, k, k // 2, k % 2)
                            beside.dve_end(v)

                    @block.sync
                    def _(sp):
                        if beside:
                            beside.sp_begin(sp)
                        with sp.Fori(0, NT) as i:
                            for x in range(4):
                                sp.wait_ge(by_act, 8 * i + (2 * x + 4))
                                sp.wait_ge(by_dve, 8 * i + (2 * x + 4))
                                sp.dma_start(rows[i, :, x, :], cube[:, x, :, :, :, :].rearrange("p z y a b -> p (z y a b)")).then_inc(stored[x], 16)
                        for x in range(4):
                            sp.wait_ge(stored[x], 16 * NT)

        def spline(name, f, table, result, tables=None):
            with Phase():
                weight, cidx = tables or corner_buffers(name)
                if tables is None:
                    with Phase():
                        i0 = sb(name + "_i0", [P, T, D])
                        fr = sb(name + "_fr", [P, T, D])
                        fr0 = sb(name + "_fr0", [P, T, D])
                        tmp = sb(name + "_tmp", [P, T])
                        step = sem(name + "_step")
                        with nc.Block() as block:

                            @block.vector
                            def _(v):
                                corner_tables(v, Chain(v, step), i0, fr, fr0, weight, cidx, tmp, bass.ds(0, T))

                stage = sb(name + "_stage", [P, 2, HALF], I32)
                rows = sb(name + "_rows", [P, 2, HALF, 8 * f])
                parts = sb(name + "_parts", [P, 2, HALF, 8, f])
                msg = sb(name + "_msg", [P, 2, HALF, f])
                own = sb(name + "_own", [P, 2, HALF, P])
                sums_ps = ps(name + "_sums_ps", [P, NT * f])
                staged, weighted, made, used, gate, gate_a, summed = (sem(name + x) for x in ("_staged", "_weighted", "_made", "_used", "_gate", "_gate_a", "_summed"))
                fetched = [sem(f"{name}_fetched{g}") for g in range(2)]
                with nc.Block() as block:

                    @block.gpsimd
                    def _(pool):
                        with pool.Fori(0, TRIPS) as i:
                            for g in range(2):
                                pool.wait_ge(staged, 2 * i + g + 1)
                                pool.sem_inc(gate, 1)
                                for j in range(HALF):
                                    pool.indirect_dma_start(rows[:, g, j, :], None, table,
                                                            bass.IndirectOffsetOnAxis(ap=stage[:, g, j:j + 1], axis=0)).then_inc(fetched[g], 16)

                    @block.scalar
                    def _(act):
                        def put(n, g):
                            act.activation(stage[:, g, :], cidx[:, bass.ds(n * HALF, HALF)], ACT.Copy).then_inc(staged, 1)

                        put(0, 0)
                        put(1, 1)
                        with act.Fori(0, TRIPS - 1) as i:
                            for g in range(2):
                                act.wait_ge(fetched[g], (i + 1) * (HALF * 16))
                                act.wait_ge(weighted, 2 * i + g + 1)
                                act.sem_inc(gate_a, 1)
                                put(2 * i + g + 2, g)

                    @block.vector
                    def _(v):
                        def weigh(n, trip, g):
                            s = bass.ds(n * HALF, HALF)
                            v.wait_ge(fetched[g], (trip + 1) * (HALF * 16))
                            v.tensor_tensor(parts[:, g, :, :, :].rearrange("p t s o -> p (t s) o"),
                                            rows[:, g, :, :].rearrange("p t (s o) -> p (t s) o", o=f),
                                            bcast(weight[:, s, :].rearrange("p t s -> p (t s)"), 2, f), ALU.mult).then_inc(weighted, 1)

                        def add_up(n, g):
                            s = bass.ds(n * HALF, HALF)
                            v.wait_ge(used, n + 1)
                            v.tensor_tensor(own[:, g, :, :], bcast(iota128[:, :], 1, HALF), bcast(srclo[:, s], 2, P), ALU.is_equal)
                            v.wait_ge(weighted, n + 1)
                            v.tensor_reduce(msg[:, g, :, :], parts[:, g, :, :, :].rearrange("p t s o -> p t o s"), AX, ALU.add).then_inc(made, 1)

                        with v.Fori(0, TRIPS) as i:
                            for g in range(2):
                                weigh(2 * i + g, i, g)
                                add_up(2 * i + g, g)
                        v.wait_ge(summed, 1)
                        v.tensor_tensor(result, sums_ps[:, :].rearrange("p (t o) -> p t o", t=NT), bcast(rdeg[:, :], 2, f), ALU.mult)

                    @block.tensor
                    def _(pe):
                        clear(pe, sums_ps, NT * f)
                        pe.sem_inc(used, 2)
                        with pe.Fori(0, TRIPS) as i:
                            for g in range(2):
                                n = 2 * i + g
                                tiles = buckets(bucket, n)
                                pe.wait_ge(made, n + 1)
                                for j in range(HALF):
                                    last = pe.matmul(sums_ps[:, bass.ds(tiles[j] * f, f)], own[:, g, j, :], msg[:, g, j, :],
                                                     start=False, stop=False, skip_group_check=True)
                                last.then_inc(used, 1)
                        close(pe, sums_ps, NT * f).then_inc(summed, 1)

        with Phase():
            w1s = sb("w1s", [K, H1])
            w3s = sb("w3s", [H1, H1])
            w4s = sb("w4s", [H1, D])
            bias = sb("bias", [P, 4, H1])
            tn = sb("tn", [P, 2, NT, D])
            with Phase():
                sums = sb("sums", [P, NT, K + 1])
                with Phase():
                    hat = sb("hat", [P, T, D, KS])
                    deg = sb("deg", [P, NT])
                    rec_deg = sb("rec_deg", [P, NT])
                    nt_tmp = sb("nt_tmp", [P, NT])
                    has = sb("has", [P, NT])
                    with Phase():
                        back = sb("back", [P, T, REC])
                        ti = sb("ti", [P, T], I32)
                        t2 = sb("t2", [P, T], I32)
                        loaded, step = sem("loaded2"), sem("step2")
                        with nc.Block() as block:

                            @block.sync
                            def _(sp):
                                sp.dma_start(back[:, :, :].rearrange("p t r -> p (t r)"), recs.rearrange("(p t) r -> p (t r)", p=P)).then_inc(loaded, 16)

                            @block.vector
                            def _(v):
                                ch = Chain(v, step)
                                v.wait_ge(loaded, 16)
                                v.tensor_copy(edst[:, :], back[:, :, 1])
                                v.tensor_copy(pseudo[:, :, :], back[:, :, 2:2 + D])
                                ch.link(v.tensor_copy(ti[:, :], back[:, :, 0]))
                                ch.link(v.tensor_scalar(ti[:, :], ti[:, :], P - 1, None, ALU.bitwise_and))
                                ch.link(v.tensor_copy(srclo[:, :], ti[:, :]))
                                ch.link(v.tensor_scalar(dsthi[:, :], back[:, :, 0], 0.0, 1024.0, ALU.min, ALU.mult))
                                ch.link(v.tensor_tensor(srclo[:, :], srclo[:, :], dsthi[:, :], ALU.add))
                                ch.link(v.tensor_copy(ti[:, :], back[:, :, 1]))
                                ch.link(v.tensor_scalar(t2[:, :], ti[:, :], 7, None, ALU.arith_shift_right))
                                ch.link(v.tensor_scalar(ti[:, :], ti[:, :], P - 1, None, ALU.bitwise_and))
                                v.tensor_copy(dstlo[:, :], ti[:, :])
                                ch.link(v.tensor_copy(dsthi[:, :], t2[:, :]))
                                for k in range(KS):
                                    ch.link(v.tensor_scalar(hat[:, :, :, k], pseudo[:, :, :], float(KS - 1), -float(k), ALU.mult, ALU.add))
                                hf = hat[:, :, :, :].rearrange("p t d k -> p (t d k)")
                                ch.link(v.scalar_tensor_tensor(hf, hf, -1.0, hf, ALU.mult, ALU.min))
                                ch.link(v.tensor_scalar(hf, hf, 1.0, 0.0, ALU.add, ALU.max))

                    yz = sb("yz", [P, 2, HALF, KS, KS])
                    basis = sb("basis", [P, 2, HALF, K + 1])
                    own = sb("own", [P, 2, HALF, P])
                    dlo = sb("dlo", [P, 2, HALF, P], BF16)
                    dhi = sb("dhi", [P, 2, HALF, NT], BF16)
                    stage_dst, store_dst = scatter("by_dst", dposi, drec, DREC, drecs)
                    sums_ps = ps("sums_ps", [P, NT * P])
                    deg_ps = ps("deg_ps", [P, BANK])
                    made, used, step, summed, turn, loaded = (sem(n) for n in ("made", "used", "step3", "summed", "turn3", "loaded3"))
                    with nc.Block() as block:

                        @block.sync
                        def _(sp):
                            sp.dma_start(w1s[:, :], w1.rearrange("k i o -> k (i o)")).then_inc(loaded, 16)
                            sp.dma_start(w3s[:, :], w3).then_inc(loaded, 16)
                            sp.dma_start(w4s[:, :], w4).then_inc(loaded, 16)
                            for n, (b, width) in enumerate(((b1, H1), (b2, H1), (b3, H1), (b4, D))):
                                sp.dma_start(bias[:, n, 0:width], b.partition_broadcast(P)).then_inc(loaded, 16)
                            sp.wait_ge(loaded, 7 * 16)

                        @block.gpsimd
                        def _(pool):
                            store_dst(pool)

                        @block.vector
                        def _(v):
                            ch = Chain(v, step)
                            ch.link(v.memset(basis[:, :, :, K:K + 1], 1.0))
                            base = ch.k

                            def make(i, g):
                                n = 2 * i + g
                                ch.off, ch.k = base + n, 0
                                v.wait_ge(used, n + 1)
                                s = bass.ds(n * HALF, HALF)
                                hx, hy, hz = (hat[:, s, d, :] for d in range(D))
                                ch.link(v.tensor_tensor(yz[:, g, :, :, :], bcast(hy, 3, KS), bcast(hz, 2, KS), ALU.mult))
                                yzf = yz[:, g, :, :, :].rearrange("p t y z -> p t (y z)")
                                v.tensor_tensor(basis[:, g, :, 0:K].rearrange("p t (x r) -> p t x r", x=KS),
                                                bcast(hx, 3, KS * KS), bcast(yzf, 2, KS), ALU.mult)
                                v.tensor_tensor(dhi[:, g, :, :], bcast(iota128[:, 0:NT], 1, HALF), bcast(dsthi[:, s], 2, NT), ALU.is_equal)
                                v.tensor_tensor(dlo[:, g, :, :], bcast(iota128[:, :], 1, HALF), bcast(dstlo[:, s], 2, P), ALU.is_equal)
                                v.tensor_tensor(own[:, g, :, :], bcast(iota128[:, :], 1, HALF), bcast(srclo[:, s], 2, P), ALU.is_equal).then_inc(made, 1)

                            with v.Fori(0, TRIPS) as i:
                                make(i, 0)
                                make(i, 1)
                            ch.off, ch.k = base + 2 * TRIPS, 0
                            v.wait_ge(summed, 1)
                            ch.link(v.tensor_copy(sums[:, :, :], sums_ps[:, :].rearrange("p (t k) -> p t k", t=NT)[:, :, 0:K + 1]))
                            v.tensor_scalar(rdeg[:, :], sums[:, :, K], 1.0, None, ALU.max)
                            ch.link(v.tensor_scalar(deg[:, :], deg_ps[:, 0:NT], 1.0, None, ALU.max))
                            v.tensor_scalar(has[:, :], deg_ps[:, 0:NT], 0.0, None, ALU.is_gt)
                            ch.link(v.reciprocal(rdeg[:, :], rdeg[:, :]))
                            v.reciprocal(rec_deg[:, :], deg[:, :]).then_inc(turn, 1)
                            v.wait_ge(turn, 2)
                            refine(v, ch, dis[:, :], deg[:, :], nt_tmp[:, :])
                            v.tensor_tensor(dis[:, :], dis[:, :], has[:, :], ALU.mult)

                        @block.scalar
                        def _(act):
                            stage_dst(act)
                            act.wait_ge(turn, 1)
                            act.activation(dis[:, :], rec_deg[:, :], ACT.Sqrt).then_inc(turn, 1)

                        @block.tensor
                        def _(pe):
                            pe.matmul(deg_ps[:, 0:NT], zeros[:, 0:P], zeros[:, 0:NT], start=True, stop=False)
                            clear(pe, sums_ps, NT * P)
                            pe.sem_inc(used, 2)

                            def add(n, g):
                                tiles = buckets(bucket, n)
                                pe.wait_ge(made, n + 1)
                                for j in range(HALF):
                                    pe.matmul(deg_ps[:, 0:NT], dlo[:, g, j, :], dhi[:, g, j, :], start=False, stop=False)
                                    last = pe.matmul(sums_ps[:, bass.ds(tiles[j] * P, K + 1)], own[:, g, j, :], basis[:, g, j, :],
                                                     start=False, stop=False, skip_group_check=True)
                                last.then_inc(used, 1)

                            with pe.Fori(0, TRIPS) as i:
                                add(2 * i, 0)
                                add(2 * i + 1, 1)
                            pe.matmul(deg_ps[:, 0:NT], zeros[:, 0:P], zeros[:, 0:NT], start=False, stop=True)
                            close(pe, sums_ps, NT * P).then_inc(summed, 1)

                with Phase():
                    loaded, step = sem("loaded5"), sem("step5")
                    with nc.Block() as block:

                        @block.vector
                        def _(v):
                            v.memset(xn[:, :, :], 0.0).then_inc(step, 1)

                        @block.sync
                        def _(sp):
                            sp.wait_ge(step, 1)
                            sp.dma_start(xn[:, 0:NT - 1, :], x[0:(NT - 1) * P, :].rearrange("(t p) c -> p t c", p=P)).then_inc(loaded, 16)
                            sp.dma_start(xn[0:NREST, NT - 1, :], x[(NT - 1) * P:N, :]).then_inc(loaded, 16)
                            sp.wait_ge(loaded, 32)

                norm_relu("n0", xn[:, :, :], cur[:, :, :])
                with Phase():
                    loaded, step = sem("loaded6"), sem("step6")
                    dlow = sb("dlow", [P, T], I32)
                    with nc.Block() as block:

                        @block.sync
                        def _(sp):
                            sp.dma_start(dback[:, :, :].rearrange("p t r -> p (t r)"), drecs.rearrange("(p t) r -> p (t r)", p=P)).then_inc(loaded, 16)

                        @block.vector
                        def _(v):
                            ch = Chain(v, step)
                            v.tensor_copy(total[:, :, :], cur[:, :, :])
                            v.wait_ge(loaded, 16)
                            v.tensor_scalar(gsrc[:, :], dback[:, :, 0], 0.0, None, ALU.max)
                            ch.link(v.tensor_copy(dlow[:, :], dback[:, :, 1]))
                            ch.link(v.tensor_scalar(dlow[:, :], dlow[:, :], P - 1, None, ALU.bitwise_and))
                            ch.link(v.tensor_copy(dback[:, :, 0], dlow[:, :]))
                            ch.link(v.tensor_scalar(dback[:, :, 1], dback[:, :, 1], 0.0, 1024.0, ALU.min, ALU.mult))
                            ch.link(v.tensor_tensor(dback[:, :, 0], dback[:, :, 0], dback[:, :, 1], ALU.add))

                linear("l1", lambda t: sums[:, t, 0:K], K, w1s[:, :], H1, h, scale=rdeg)
            bias_elu("e1", h[:, :, :], bias[:, 0, :])
            build_corners("z2", H1, h, w2, corners2, layer=0)
            spline("s2", H1, corners2, h[:, :, :])
            bias_elu("e2", h[:, :, :], bias[:, 1, :])
            linear("l3", lambda t: h[:, t, :], H1, w3s[:, :], H1, h)
            bias_elu("e3", h[:, :, :], bias[:, 2, :])
            linear("l4", lambda t: h[:, t, :], H1, w4s[:, :], D, tn[:, 0, :, :])

            QUAD = 4
            GROUPS = T // QUAD
            own = sb("own4", [P, 2, 2, QUAD, P], BF16)
            pick = sb("pick", [P, 2, 2, QUAD * P], BF16)
            which = sb("which", [P, 2, 2, QUAD, NT])
            masked = sb("masked", [P, 2, QUAD, D, 2, NT])
            diff = sb("diff", [P, T, D])
            ident16 = sb("ident16", [P, P], BF16)
            rest = sb("rest", [P, 2, NT, D])
            tparts = sb("tparts", [P, 3, 2, NT * D], BF16)
            pick_ps = ps("pick_ps", [P, 2, 2, QUAD * P], BF16)
            all_ps = ps("all_ps", [P, 2, 2, BANK])
            made, turned, copied, picked, step, masks, split = (sem(n) for n in ("made4", "turned4", "copied4", "picked4", "step4", "masks4", "split4"))
            taken, totaled = sem("taken4"), sem("totaled4")
            beside = Layer(1)
            with nc.Block() as block:

                @block.sync
                def _(sp):
                    beside.sp_begin(sp)

                @block.gpsimd
                def _(pool):
                    beside.pool_begin(pool)
                    with pool.Fori(0, TRIPS) as i:
                        for g in range(2):
                            beside.pool(pool, 2 * i + g, i, g)

                @block.vector
                def _(v):
                    beside.dve_begin(v)
                    ch = Chain(v, step)
                    v.tensor_copy(ident16[:, :], ident[:, :])
                    ch.link(v.tensor_tensor(tn[:, 0, :, :], tn[:, 0, :, :], bcast(bias[:, 3, 0:D], 1, NT), ALU.add))
                    ch.link(v.tensor_scalar(tn[:, 1, :, :], tn[:, 0, :, :], -1.0, None, ALU.mult))
                    tf, rf = (a[:, :, :, :].rearrange("p s t c -> p s (t c)") for a in (tn, rest))
                    for q in range(3):
                        ch.link(v.tensor_copy(tparts[:, q, :, :], tf))
                        ch.link(v.tensor_copy(rf, tparts[:, q, :, :]))
                        ch.link(v.tensor_tensor(tf, tf, rf, ALU.subtract))
                    v.sem_inc(split, 1)

                    def make(n, g):
                        v.wait_ge(turned, n + 1)
                        s = bass.ds(n * QUAD, QUAD)
                        it = bcast(iota128[:, :], 1, QUAD)
                        v.tensor_tensor(own[:, g, 0, :, :], it, bcast(dstlo[:, s], 2, P), ALU.is_equal)
                        v.tensor_tensor(own[:, g, 1, :, :], it, bcast(srclo[:, s], 2, P), ALU.is_equal).then_inc(made, 1)

                    def take(n, g):
                        s = bass.ds(n * QUAD, QUAD)
                        v.wait_ge(taken, n + 1)
                        it = bcast(iota128[:, 0:NT], 1, QUAD)
                        v.tensor_tensor(which[:, g, 0, :, :], it, bcast(dsthi[:, s], 2, NT), ALU.is_equal)
                        v.tensor_tensor(which[:, g, 1, :, :], it, bcast(bucket[:, s], 2, NT), ALU.is_equal).then_inc(masks, 1)
                        v.wait_ge(picked, n + 3)
                        v.wait_ge(masks, n + 1)
                        v.wait_ge(totaled, n + 1)
                        for side in range(2):
                            a = all_ps[:, g, side, 0:QUAD * NT * D].rearrange("p (j b c) -> p j b c", j=QUAD, b=NT)
                            m = masked[:, g, :, :, side, :].rearrange("p j c b -> p j b c")
                            last = v.tensor_tensor(m, a, bcast(which[:, g, side, :, :], 3, D), ALU.mult)
                        last.then_inc(taken, 1)

                    def add_up(n, g):
                        v.wait_ge(taken, n + 3)
                        v.tensor_reduce(diff[:, bass.ds(n * QUAD, QUAD), :].rearrange("p t c -> p (t c)"),
                                        masked[:, g, :, :, :, :].rearrange("p j c s b -> p (j c) (s b)"), AX, ALU.add).then_inc(totaled, 1)

                    def turn(m, k):
                        make(m + 2, k % 2)
                        add_up(m - 1, (k + 1) % 2)
                        take(m, k % 2)

                    make(0, 0)
                    make(1, 1)
                    make(2, 0)
                    take(0, 0)
                    with v.Fori(0, TRIPS - 1) as i:
                        for k in range(4):
                            if k % 2 == 0:
                                beside.dve(v, 2 * i + k // 2, i, k // 2)
                            turn(4 * i + k + 1, k + 1)
                    turn(GROUPS - 3, 1)
                    add_up(GROUPS - 3, 1)
                    take(GROUPS - 2, 0)
                    add_up(GROUPS - 2, 0)
                    take(GROUPS - 1, 1)
                    add_up(GROUPS - 1, 1)
                    for g in range(2):
                        beside.dve(v, HALVES - 2 + g, TRIPS - 1, g)
                    v.wait_ge(totaled, 2 + GROUPS)
                    ch.link(v.tensor_tensor(pseudo[:, :, :], pseudo[:, :, :], diff[:, :, :], ALU.add))
                    v.tensor_scalar(pseudo[:, :, :], pseudo[:, :, :], 0.0, 1.0, ALU.max, ALU.min)
                    beside.dve_end(v)

                @block.tensor
                def _(pe):
                    beside.pe_begin(pe)
                    pe.sem_inc(turned, 2)
                    pe.wait_ge(split, 1)

                    def turn(n, g):
                        pe.wait_ge(copied, n + 1)
                        pe.wait_ge(made, n + 1)
                        for side in range(2):
                            for j in range(QUAD):
                                last = pe.transpose(pick_ps[:, g, side, j * P:(j + 1) * P], own[:, g, side, j, :], ident16[:, :])
                        last.then_inc(turned, 1)

                    def select(n, g):
                        pe.wait_ge(copied, n + 3)
                        pe.wait_ge(taken, n + 1)
                        for side in range(2):
                            for j in range(QUAD):
                                for q in range(3):
                                    last = pe.matmul(all_ps[:, g, side, j * NT * D:(j + 1) * NT * D], pick[:, g, side, j * P:(j + 1) * P],
                                                     tparts[:, q, side, :], start=q == 0, stop=q == 2)
                        last.then_inc(picked, 1)

                    turn(0, 0)
                    with pe.Fori(0, TRIPS - 1) as i:
                        for k in range(4):
                            turn(4 * i + k + 1, (k + 1) % 2)
                            select(4 * i + k, k % 2)
                            if k % 2:
                                beside.pe(pe, 2 * i + k // 2, i, k // 2)
                    for k in range(GROUPS - 4, GROUPS):
                        if k + 1 < GROUPS:
                            turn(k + 1, (k + 1) % 2)
                        select(k, k % 2)
                    for g in range(2):
                        beside.pe(pe, HALVES - 2 + g, TRIPS - 1, g)
                    beside.pe_end(pe)

                @block.scalar
                def _(act):
                    act.sem_inc(copied, 2)
                    act.sem_inc(taken, 2)
                    act.sem_inc(totaled, 2)
                    act.sem_inc(picked, 2)
                    beside.act_begin(act)

                    def copy(n, g):
                        act.wait_ge(picked, n + 1)
                        act.wait_ge(turned, n + 3)
                        act.activation(pick[:, g, :, :], pick_ps[:, g, :, :], ACT.Copy).then_inc(copied, 1)

                    with act.Fori(0, TRIPS - 1) as i:
                        for k in range(4):
                            copy(4 * i + k, k % 2)
                            if k % 2:
                                beside.act(act, 2 * i + k // 2, i, k // 2)
                    for k in range(GROUPS - 4, GROUPS):
                        copy(k, k % 2)

        with Phase():
            tables = corner_buffers("s3")
            propagate(2, *tables)

            norm_relu("n1", xn[:, :, :], h[:, :, 0:C])
            build_corners("z3", C, h, wc, corners3)
            spline("s3", C, corners3, h[:, :, 0:C], tables)
        with Phase():
            bias3 = sb("bias3", [P, C])
            loaded, step, ready = sem("loaded7"), sem("step7"), sem("ready7")
            with nc.Block() as block:

                @block.vector
                def _(v):
                    ch = Chain(v, step)
                    r = h[:, :, 0:C]
                    v.wait_ge(loaded, 16)
                    ch.link(v.tensor_tensor(r, r, bcast(bias3[:, :], 1, NT), ALU.add))
                    v.tensor_tensor(xn[:, :, :], xn[:, :, :], r, ALU.add).then_inc(ready, 1)

                @block.sync
                def _(sp):
                    sp.dma_start(bias3[:, :], bc.partition_broadcast(P)).then_inc(loaded, 16)
                    sp.wait_ge(ready, 1)
                    sp.dma_start(out[0:(NT - 1) * P, :].rearrange("(t p) c -> p t c", p=P), xn[:, 0:NT - 1, :]).then_inc(loaded, 16)
                    sp.dma_start(out[(NT - 1) * P:N, :], xn[0:NREST, NT - 1, :]).then_inc(loaded, 16)
                    sp.wait_ge(loaded, 48)


_INS = ['x', 'src', 'dst', 'edge_attr_3', 'L1_gnn_stn1_w', 'L1_gnn_stn1_b', 'L1_gnn_stn2_w', 'L1_gnn_stn2_b',
        'L1_gnn_stn3_w', 'L1_gnn_stn3_b', 'L1_gnn_stn4_w', 'L1_gnn_stn4_b', 'L1_gnn_conv_w', 'L1_gnn_conv_b']
_OUTS = [((N, C), 'float32')]


def kernel(**inputs):
    import numpy as _np
    import concourse.bacc as _bacc
    from concourse import mybir as _mybir
    from concourse.bass_utils import run_bass_kernel_spmd as _run

    nc = _bacc.Bacc("TRN2", target_bir_lowering=False, num_devices=1)
    arrays, args = {}, []
    for name in _INS:
        a = _np.ascontiguousarray(inputs[name])
        arrays[f"in_{name}_dram"] = a
        args.append(nc.dram_tensor(f"in_{name}_dram", a.shape, _mybir.dt.from_np(a.dtype), kind="ExternalInput").ap())
    for i, (shape, dtype) in enumerate(_OUTS):
        dt = _mybir.dt.from_np(_np.dtype(dtype))
        args.append(nc.dram_tensor(f"out_{i}_dram", shape, dt, kind="ExternalOutput").ap())
    gnn(nc, *args)
    r = _run(nc, [arrays], core_ids=[0])
    got = tuple(r.results[0][f"out_{i}_dram"] for i in range(len(_OUTS)))
    return got[0]
```
